# Optimizing a Trainium2 kernel written in Bass

```python
import numpy as np
import jax
import jax.numpy as jnp

def _softmax(x, axis=-1):
    return jax.nn.softmax(x, axis=axis)

def _gelu(x):
    return jax.nn.gelu(x, approximate=True)

def _silu(x):
    return jax.nn.silu(x)

def _sigmoid(x):
    return jax.nn.sigmoid(x)

def _layernorm(x, axis=-1, eps=1e-05):
    m = jnp.mean(x, axis=axis, keepdims=True)
    v = jnp.var(x, axis=axis, keepdims=True)
    return (x - m) / jnp.sqrt(v + eps)

def _scatter_add(tgt, idx, src, axis=0):
    return tgt.at[idx].add(src)

def _segment_sum(src, seg, n):
    return jax.ops.segment_sum(src, seg, n)
kernel_name = 'mk_flamingo_gated_d2_seqx_r4_63732e'

def setup_inputs(seed: int=0):
    np.random.seed(seed)
    _w = jnp.asarray

    def _rec_inputs():
        import jax
        import jax.numpy as jnp
        _rk = jax.random.key(seed)
        x = -0.0003929 + 0.9999 * jax.random.normal(jax.random.fold_in(_rk, 1), (4, 1024, 256), jnp.float32)
        _lenS = 1024 - jax.random.randint(jax.random.fold_in(_rk, 7), (4,), 0, max(1, 1024 // 4) + 1, jnp.int32)
        _lenS2 = 77 - jax.random.randint(jax.random.fold_in(_rk, 8), (4,), 0, max(1, 77 // 4) + 1, jnp.int32)
        _ctx_1024P = jax.random.normal(jax.random.fold_in(_rk, 11), (4, 16, 256), jnp.float32)
        _ctx_1024c = jax.random.dirichlet(jax.random.fold_in(_rk, 511), 0.3 * jnp.ones((16,), jnp.float32), (4, 77))
        _ctx_1024t = jnp.einsum('bsk,bkd->bsd', _ctx_1024c, _ctx_1024P)
        _ctx_1024t = _ctx_1024t * jax.lax.rsqrt(jnp.mean(jnp.square(_ctx_1024t)) + 1e-12) * 0.953939
        ctx_1024 = 2.81802e-05 + 1.00001 * (_ctx_1024t + 0.3 * jax.random.normal(jax.random.fold_in(_rk, 611), (4, 77, 256), jnp.float32))
        _validS = jnp.arange(1024)[None, :] < _lenS[:, None]
        _validS2 = jnp.arange(77)[None, :] < _lenS2[:, None]
        _causal = jnp.tril(jnp.ones((1024, 1024), dtype=bool))
        mask_BxS2_ik1 = jnp.where(jnp.broadcast_to(_validS2[:, :], (4, 77)), 1, 0).astype(jnp.int32)
        _g = jax.random.normal(jax.random.fold_in(_rk, 9001), (2, 2), jnp.float32)
        _g = jnp.sign(_g) * jnp.maximum(jnp.abs(_g), 1.0) + (_g == 0) * 1.0
        g_xattn = _g[0]
        g_ffn = _g[1]
        return (x, ctx_1024, mask_BxS2_ik1, g_xattn, g_ffn)
    x, ctx_1024, mask_BxS2_ik1, g_xattn, g_ffn = _rec_inputs()

    def _L0_xattn_setup():
        import jax, jax.numpy as jnp
        import numpy as np
        NEG_INF = -10000000000.0
        key = jax.random.key(seed)
        k1, k2, k3, k4 = jax.random.split(key, 4)
        B, Lq, Lk, D = (8, 512, 512, 256)
        hidden = jax.random.normal(k1, (B, Lq, D), dtype=jnp.float32)
        keys = jax.random.normal(k2, (B, Lk, D), dtype=jnp.float32)
        values = jax.random.normal(k3, (B, Lk, D), dtype=jnp.float32)
        mask = jax.random.randint(k4, (B, Lk), 0, 2, dtype=jnp.int32)
        return {'hidden': hidden, 'keys': keys, 'values': values, 'mask': mask}
    _L0_xattn_all = _L0_xattn_setup()
    _L0_xattn_in = {k: v for k, v in _L0_xattn_all.items() if k in ()}
    del _L0_xattn_all

    def _L0_ffn_setup():
        import jax, jax.numpy as jnp
        import numpy as np
        DIM = 256
        INTER = 256
        E = 8
        TOPK = 2
        ROUTE_SCALE = 1.0
        SHARED_INTER = 512
        B, S = (4, 512)

        def _moe_forward(x, gate_w, gate_b, w1, b1, w3, b3, w2, b2, ws1, bs1, ws3, bs3, ws2, bs2):
            Bq, Sq, D = x.shape
            xt = x.reshape(-1, D)
            logits = (xt @ gate_w.T + gate_b).astype(jnp.float32)
            scores = jax.nn.softmax(logits, axis=-1)
            top_w, top_i = jax.lax.top_k(scores, TOPK)
            weights = (top_w * ROUTE_SCALE).astype(x.dtype)
            gate_dense = jnp.sum(jax.nn.one_hot(top_i, E, dtype=x.dtype) * weights[..., None], axis=1)

            def expert(w1e, b1e, w3e, b3e, w2e, b2e):
                h = jax.nn.silu(xt @ w1e.T + b1e) * (xt @ w3e.T + b3e)
                return h @ w2e.T + b2e
            outs = jax.vmap(expert)(w1, b1, w3, b3, w2, b2)
            y = jnp.einsum('etd,te->td', outs, gate_dense)
            z = jax.nn.silu(xt @ ws1.T + bs1) * (xt @ ws3.T + bs3) @ ws2.T + bs2
            return (y + z).reshape(Bq, Sq, D)
        key = jax.random.key(seed)
        ks = jax.random.split(key, 10)

        def w(k, shape, scale=0.02):
            return jax.random.normal(k, shape, jnp.float32) * scale
        return {'x': jax.random.normal(ks[0], (B, S, DIM), jnp.float32), 'gate_w': w(ks[1], (E, DIM)), 'gate_b': jnp.zeros((E,), jnp.float32), 'w1': w(ks[2], (E, INTER, DIM)), 'b1': jnp.zeros((E, INTER), jnp.float32), 'w3': w(ks[3], (E, INTER, DIM)), 'b3': jnp.zeros((E, INTER), jnp.float32), 'w2': w(ks[4], (E, DIM, INTER)), 'b2': jnp.zeros((E, DIM), jnp.float32), 'ws1': w(ks[5], (SHARED_INTER, DIM)), 'bs1': jnp.zeros((SHARED_INTER,), jnp.float32), 'ws3': w(ks[6], (SHARED_INTER, DIM)), 'bs3': jnp.zeros((SHARED_INTER,), jnp.float32), 'ws2': w(ks[7], (DIM, SHARED_INTER)), 'bs2': jnp.zeros((DIM,), jnp.float32)}
    _L0_ffn_all = _L0_ffn_setup()
    _L0_ffn_in = {k: v for k, v in _L0_ffn_all.items() if k in ('gate_w', 'gate_b', 'w1', 'b1', 'w3', 'b3', 'w2', 'b2', 'ws1', 'bs1', 'ws3', 'bs3', 'ws2', 'bs2')}
    del _L0_ffn_all

    def _L1_xattn_setup():
        import jax, jax.numpy as jnp
        import numpy as np
        D_MODEL = 256
        NUM_HEADS = 16
        D_HEAD = D_MODEL // NUM_HEADS
        key = jax.random.key(seed)
        ks = jax.random.split(key, 11)
        B, S = (4, 512)
        s_in = 1.0 / np.sqrt(D_MODEL)
        s_out = 1.0 / np.sqrt(NUM_HEADS * D_HEAD)
        return {'Q': jax.random.normal(ks[0], (B, S, D_MODEL), jnp.float32), 'K': jax.random.normal(ks[1], (B, S, D_MODEL), jnp.float32), 'V': jax.random.normal(ks[2], (B, S, D_MODEL), jnp.float32), 'Wq': jax.random.uniform(ks[3], (D_MODEL, D_HEAD), jnp.float32, -s_in, s_in), 'bq': jax.random.uniform(ks[4], (D_HEAD,), jnp.float32, -s_in, s_in), 'Wk': jax.random.uniform(ks[5], (D_MODEL, D_HEAD), jnp.float32, -s_in, s_in), 'bk': jax.random.uniform(ks[6], (D_HEAD,), jnp.float32, -s_in, s_in), 'Wv': jax.random.uniform(ks[7], (D_MODEL, D_HEAD), jnp.float32, -s_in, s_in), 'bv': jax.random.uniform(ks[8], (D_HEAD,), jnp.float32, -s_in, s_in), 'Wo': jax.random.uniform(ks[9], (NUM_HEADS * D_HEAD, D_MODEL), jnp.float32, -s_out, s_out), 'bo': jax.random.uniform(ks[10], (D_MODEL,), jnp.float32, -s_out, s_out)}
    _L1_xattn_all = _L1_xattn_setup()
    _L1_xattn_in = {k: v for k, v in _L1_xattn_all.items() if k in ('Wq', 'bq', 'Wk', 'bk', 'Wv', 'bv', 'Wo', 'bo')}
    del _L1_xattn_all

    def _L1_ffn_setup():
        import jax, jax.numpy as jnp
        import numpy as np
        DIM = 256
        HIDDEN = 768
        SCALE = 1.0 / 127.0

        def _dequant(w_int, dtype):
            return w_int.astype(dtype) * jnp.asarray(SCALE, dtype)
        key = jax.random.key(seed)
        k_x, k_g, k_u, k_d = jax.random.split(key, 4)
        x = jax.random.normal(k_x, (4, 512, DIM), dtype=jnp.float32)
        w_gate = jax.random.randint(k_g, (HIDDEN, DIM), -127, 128, dtype=jnp.int32)
        w_up = jax.random.randint(k_u, (HIDDEN, DIM), -127, 128, dtype=jnp.int32)
        w_down = jax.random.randint(k_d, (DIM, HIDDEN), -127, 128, dtype=jnp.int32)
        return {'x': x, 'w_gate': w_gate, 'w_up': w_up, 'w_down': w_down}
    _L1_ffn_all = _L1_ffn_setup()
    _L1_ffn_in = {k: v for k, v in _L1_ffn_all.items() if k in ('w_gate', 'w_up', 'w_down')}
    del _L1_ffn_all
    return {'x': x, 'ctx_1024': ctx_1024, 'mask_BxS2_ik1': mask_BxS2_ik1, 'g_xattn': g_xattn, 'g_ffn': g_ffn, 'L0_ffn_gate_w': _L0_ffn_in['gate_w'], 'L0_ffn_gate_b': _L0_ffn_in['gate_b'], 'L0_ffn_w1': _L0_ffn_in['w1'], 'L0_ffn_b1': _L0_ffn_in['b1'], 'L0_ffn_w3': _L0_ffn_in['w3'], 'L0_ffn_b3': _L0_ffn_in['b3'], 'L0_ffn_w2': _L0_ffn_in['w2'], 'L0_ffn_b2': _L0_ffn_in['b2'], 'L0_ffn_ws1': _L0_ffn_in['ws1'], 'L0_ffn_bs1': _L0_ffn_in['bs1'], 'L0_ffn_ws3': _L0_ffn_in['ws3'], 'L0_ffn_bs3': _L0_ffn_in['bs3'], 'L0_ffn_ws2': _L0_ffn_in['ws2'], 'L0_ffn_bs2': _L0_ffn_in['bs2'], 'L1_xattn_Wq': _L1_xattn_in['Wq'], 'L1_xattn_bq': _L1_xattn_in['bq'], 'L1_xattn_Wk': _L1_xattn_in['Wk'], 'L1_xattn_bk': _L1_xattn_in['bk'], 'L1_xattn_Wv': _L1_xattn_in['Wv'], 'L1_xattn_bv': _L1_xattn_in['bv'], 'L1_xattn_Wo': _L1_xattn_in['Wo'], 'L1_xattn_bo': _L1_xattn_in['bo'], 'L1_ffn_w_gate': _L1_ffn_in['w_gate'], 'L1_ffn_w_up': _L1_ffn_in['w_up'], 'L1_ffn_w_down': _L1_ffn_in['w_down']}

def reference(x, ctx_1024, mask_BxS2_ik1, g_xattn, g_ffn, L0_ffn_gate_w, L0_ffn_gate_b, L0_ffn_w1, L0_ffn_b1, L0_ffn_w3, L0_ffn_b3, L0_ffn_w2, L0_ffn_b2, L0_ffn_ws1, L0_ffn_bs1, L0_ffn_ws3, L0_ffn_bs3, L0_ffn_ws2, L0_ffn_bs2, L1_xattn_Wq, L1_xattn_bq, L1_xattn_Wk, L1_xattn_bk, L1_xattn_Wv, L1_xattn_bv, L1_xattn_Wo, L1_xattn_bo, L1_ffn_w_gate, L1_ffn_w_up, L1_ffn_w_down):
    import jax
    import jax.numpy as jnp

    def _L0_xattn_ref(hidden, keys, values, mask):
        import jax, jax.numpy as jnp
        import numpy as np
        NEG_INF = -10000000000.0
        scores = jnp.einsum('bqd,bkd->bqk', hidden, keys)
        scores = jnp.where(mask[:, None, :] == 0, NEG_INF, scores)
        weights = jax.nn.softmax(scores, axis=2)
        context = jnp.einsum('bqk,bkd->bqd', weights, values)
        return context

    def _L0_ffn_ref(x, gate_w, gate_b, w1, b1, w3, b3, w2, b2, ws1, bs1, ws3, bs3, ws2, bs2):
        import jax, jax.numpy as jnp
        import numpy as np
        DIM = 256
        INTER = 256
        E = 8
        TOPK = 2
        ROUTE_SCALE = 1.0
        SHARED_INTER = 512
        B, S = (4, 512)

        def _moe_forward(x, gate_w, gate_b, w1, b1, w3, b3, w2, b2, ws1, bs1, ws3, bs3, ws2, bs2):
            Bq, Sq, D = x.shape
            xt = x.reshape(-1, D)
            logits = (xt @ gate_w.T + gate_b).astype(jnp.float32)
            scores = jax.nn.softmax(logits, axis=-1)
            top_w, top_i = jax.lax.top_k(scores, TOPK)
            weights = (top_w * ROUTE_SCALE).astype(x.dtype)
            gate_dense = jnp.sum(jax.nn.one_hot(top_i, E, dtype=x.dtype) * weights[..., None], axis=1)

            def expert(w1e, b1e, w3e, b3e, w2e, b2e):
                h = jax.nn.silu(xt @ w1e.T + b1e) * (xt @ w3e.T + b3e)
                return h @ w2e.T + b2e
            outs = jax.vmap(expert)(w1, b1, w3, b3, w2, b2)
            y = jnp.einsum('etd,te->td', outs, gate_dense)
            z = jax.nn.silu(xt @ ws1.T + bs1) * (xt @ ws3.T + bs3) @ ws2.T + bs2
            return (y + z).reshape(Bq, Sq, D)
        return _moe_forward(x, gate_w, gate_b, w1, b1, w3, b3, w2, b2, ws1, bs1, ws3, bs3, ws2, bs2)

    def _L1_xattn_ref(Q, K, V, Wq, bq, Wk, bk, Wv, bv, Wo, bo):
        import jax, jax.numpy as jnp
        import numpy as np
        D_MODEL = 256
        NUM_HEADS = 16
        D_HEAD = D_MODEL // NUM_HEADS
        q = Q @ Wq + bq
        k = K @ Wk + bk
        v = V @ Wv + bv
        scores = jnp.einsum('bqd,bkd->bqk', q, k) / jnp.sqrt(jnp.float32(D_HEAD))
        attn = jax.nn.softmax(scores, axis=1)
        ctx = jnp.einsum('bqk,bkd->bqd', attn, v)
        ctx_cat = jnp.tile(ctx, (1, 1, NUM_HEADS))
        return ctx_cat @ Wo + bo

    def _L1_ffn_ref(x, w_gate, w_up, w_down):
        import jax, jax.numpy as jnp
        import numpy as np
        DIM = 256
        HIDDEN = 768
        SCALE = 1.0 / 127.0

        def _dequant(w_int, dtype):
            return w_int.astype(dtype) * jnp.asarray(SCALE, dtype)
        wg = _dequant(w_gate, x.dtype)
        wu = _dequant(w_up, x.dtype)
        wd = _dequant(w_down, x.dtype)
        gate = jnp.einsum('bsd,hd->bsh', x, wg)
        up = jnp.einsum('bsd,hd->bsh', x, wu)
        h = jax.nn.silu(gate) * up
        return jnp.einsum('bsh,dh->bsd', h, wd)
    x = x + jnp.tanh(g_xattn[0]) * _L0_xattn_ref(_layernorm(x, axis=-1), ctx_1024, ctx_1024, mask_BxS2_ik1)
    x = x + jnp.tanh(g_ffn[0]) * _L0_ffn_ref(_layernorm(x, axis=-1), L0_ffn_gate_w, L0_ffn_gate_b, L0_ffn_w1, L0_ffn_b1, L0_ffn_w3, L0_ffn_b3, L0_ffn_w2, L0_ffn_b2, L0_ffn_ws1, L0_ffn_bs1, L0_ffn_ws3, L0_ffn_bs3, L0_ffn_ws2, L0_ffn_bs2)
    x = x + jnp.tanh(g_xattn[1]) * _L1_xattn_ref(_layernorm(x, axis=-1), ctx_1024, ctx_1024, L1_xattn_Wq, L1_xattn_bq, L1_xattn_Wk, L1_xattn_bk, L1_xattn_Wv, L1_xattn_bv, L1_xattn_Wo, L1_xattn_bo)
    x = x + jnp.tanh(g_ffn[1]) * _L1_ffn_ref(_layernorm(x, axis=-1), L1_ffn_w_gate, L1_ffn_w_up, L1_ffn_w_down)
    return x

_drawn_inputs = setup_inputs


def setup_inputs(seed=0):
    import zlib

    import numpy as np

    out = dict(_drawn_inputs(seed))
    spreads = {'g_ffn': (-1.0, 0.2),
     'L0_ffn_gate_b': (0.0, 0.67),
     'L0_ffn_b1': (0.0, 0.8),
     'L0_ffn_b3': (0.0, 0.8),
     'L0_ffn_b2': (0.0, 0.39),
     'L0_ffn_bs1': (0.0, 0.8),
     'L0_ffn_bs3': (0.0, 0.8),
     'L0_ffn_bs2': (0.0, 0.314)}
    factors = {'L0_ffn_gate_w': 3.147,
     'L0_ffn_w1': 8.0,
     'L0_ffn_w3': 8.0,
     'L0_ffn_w2': 8.0,
     'L0_ffn_ws1': 2.85,
     'L0_ffn_ws3': 2.825,
     'L0_ffn_ws2': 2.718,
     'L1_xattn_Wq': 8.0,
     'L1_xattn_bq': 64.0,
     'L1_xattn_Wk': 8.0,
     'L1_xattn_bk': 8.0,
     'L1_xattn_Wv': 3.831,
     'L1_xattn_bv': 8.0,
     'L1_xattn_Wo': 4.262,
     'L1_xattn_bo': 5.006}
    for name, (base, spread) in spreads.items():
        noise = np.random.default_rng([zlib.crc32(name.encode()), seed]).standard_normal(out[name].shape)
        drawn = base * np.exp(spread * noise) if base else spread * noise
        out[name] = jnp.asarray(drawn.astype(out[name].dtype))
    for name, factor in factors.items():
        out[name] = (out[name] * factor).astype(out[name].dtype)
    return out
```

```python
from contextlib import ExitStack

import concourse.bass as bass
from concourse import mybir

B, S, D, KV = 4, 1024, 256, 77
NE, F = 8, 256
SF, LF = 512, 768
DH, NH = 16, 16
P = 128
KD = D // P
T = B * S
GT = 4
NG = T // (P * GT)
GB = NG // B
RC = T + P
NT = 2 * T // P + NE
SPARE = NE * RC
ROWS = SPARE + NE * P
MS, ML = SF // P, LF // P
EPS = 1e-5
NEG = -1e10
DEQ = 1.0 / 127.0

ALU = mybir.AluOpType
ACT = mybir.ActivationFunctionType
AX = mybir.AxisListType
F32 = mybir.dt.float32
F32R = mybir.dt.float32r
BF16 = mybir.dt.bfloat16
I32 = mybir.dt.int32
U32 = mybir.dt.uint32


def flamingo_kernel(nc, i, out):
    ctx = ExitStack()
    with ctx:
        sems = {}

        def sem(name):
            if name not in sems:
                sems[name] = ctx.enter_context(nc.semaphore(name))
            return sems[name]

        start = (nc.sbuf_base + 31) // 32 * 32

        class Area:
            def __init__(self, at, end):
                self.at, self.end = at, end

            def put(self, name, shape, dt):
                n = 1
                for s in shape[1:]:
                    n *= s
                size = (n * (2 if dt == BF16 else 4) + 31) // 32 * 32
                t = nc.alloc_sbuf_tensor_at(name, shape, dt, offset=self.at).ap()
                self.at += size
                assert self.at <= self.end, (name, self.at, self.end)
                return t

        top = nc.sbuf_usable_end // 32 * 32
        keep = Area(start, top)
        ident = keep.put("ident", [P, P], F32)
        tri = keep.put("tri", [P, P], BF16)
        onesb = keep.put("onesb", [P, P], BF16)
        onesf = keep.put("onesf", [1, P], F32)
        ones2 = keep.put("ones2", [2, P], F32R)
        ctxTm = keep.put("ctxTm", [P, B, KD, KV], F32)
        ctxr = keep.put("ctxr", [KV, B, D], F32)
        negrow = keep.put("negrow", [1, B, KV], F32)
        b13 = keep.put("b13", [2 * NE, 2 * F], F32R)
        b2 = keep.put("b2", [2 * NE, D], F32R)
        bs2 = keep.put("bs2", [2, D], F32R)
        bs13 = keep.put("bs13", [P, 2, MS], F32)
        gwh = keep.put("gwh", [P, KD, NE], F32R)
        gwl = keep.put("gwl", [P, KD, NE], F32R)
        gbias = keep.put("gbias", [P, NE], F32)
        gains = keep.put("gains", [P, 4], F32)
        fgain = keep.put("fgain", [P, 1], F32)
        halfpow = keep.put("halfpow", [P, 8], F32)
        upper16 = keep.put("upper16", [2 * NE, 2], F32)
        upper2 = keep.put("upper2", [2, 2], F32)
        expert_no = keep.put("expert_no", [P, NE], F32)
        expert_row = keep.put("expert_row", [P, NE], F32)
        pad_row = keep.put("pad_row", [P, NE], F32)
        tile_no = keep.put("tile_no", [2 * NE, NT], F32)
        incl = keep.put("incl", [NE, 2, NE], F32)
        excl = keep.put("excl", [NE, 2, NE], F32)
        rank_base = keep.put("rank_base", [P, NE], BF16)
        pos_all = keep.put("pos_all", [P, NG, 2, GT], F32)
        expert_all = keep.put("expert_all", [P, NG, 2, GT], F32)
        out_row = keep.put("out_row", [P, NG, 2, GT], U32)
        row_shift = keep.put("row_shift", [P, NE], F32)
        gate_all = keep.put("gate_all", [P, NG, 2, GT], F32)
        pick = keep.put("pick", [2 * NE, NT], F32)
        tile_expert = keep.put("tile_expert", [1, NT], I32)
        tile_row = keep.put("tile_row", [1, NT], I32)

        area_a = keep.at
        wa = Area(area_a, top)
        w13h = wa.put("w13h", [P, NE * KD, 2 * F], F32R)
        w13l = wa.put("w13l", [P, NE * KD, 2 * F], F32R)
        w2h = wa.put("w2h", [P, NE, KD * D], F32R)
        w2l = wa.put("w2l", [P, NE, KD * D], F32R)
        wsh = wa.put("wsh", [P, 6, 512], F32R)
        wsl = wa.put("wsl", [P, 6, 512], F32R)
        area_b = wa.at

        w1 = Area(area_b, top)
        xin = [w1.put(f"xin{p}", [P, GT, D], F32) for p in range(2)]
        n1 = w1.put("n1", [P, GT, D], F32)
        n1T = w1.put("n1T", [P, KD, GT * P], F32)
        probs = w1.put("probs", [P, GT, KV], F32)
        probsT = w1.put("probsT", [KV, GT * P], F32)
        stage = [w1.put(f"stage{c}", [P, 512], F32) for c in range(3)]
        area_b2 = w1.at
        x1 = [w1.put(f"x1{p}", [P, GT, D], F32) for p in range(2)]
        n2 = [w1.put(f"n2{p}", [P, GT, D], F32) for p in range(2)]
        n2Th = w1.put("n2Th", [P, KD, GT * P], F32R)
        n2Tl = w1.put("n2Tl", [P, KD, GT * P], F32R)
        sil = [w1.put(f"sil{p}", [P, 512], F32) for p in range(2)]
        hh = w1.put("hh", [P, MS, 512], F32R)
        hl = w1.put("hl", [P, MS, 512], F32R)
        negmax = w1.put("negmax", [P, GT], F32)
        psums = w1.put("psums", [P, GT], F32)
        pscale = w1.put("pscale", [P, GT], F32)
        st = [w1.put(f"st{p}", [P, GT, 6], F32) for p in range(2)]
        mv = [w1.put(f"mv{p}", [P, GT, 2], F32) for p in range(2)]
        ve = [w1.put(f"ve{p}", [P, GT], F32) for p in range(2)]
        rstd = [w1.put(f"rstd{p}", [P, GT], F32) for p in range(2)]
        logit = w1.put("logit", [P, GT, NE], F32)
        top8 = w1.put("top8", [P, GT, 8], F32)
        top8i = w1.put("top8i", [P, GT, 8], U32)
        dlog = w1.put("dlog", [P, GT, NE + 1], F32)
        elog = w1.put("elog", [P, GT, NE + 1], F32)
        esum = w1.put("esum", [P, GT], F32)
        onehot = w1.put("onehot", [P, 2, GT, NE], F32)
        routed = w1.put("routed", [P, GT, NE], BF16)
        rsum = w1.put("rsum", [P, NE], F32)
        rrow = w1.put("rrow", [P, GT, NE], F32)
        rsel = w1.put("rsel", [P, 2, GT, NE], F32)
        gatew = w1.put("gatew", [P, 2, GT], F32)
        pos = [w1.put(f"pos{p}", [P, 2, GT], U32) for p in range(2)]
        w0 = Area(area_b2, top)
        w0.put("raw_pad", [P, GT * D * 4], F32)
        b13f = w0.put("b13f", [2 * NE, 2 * F], F32)
        b2f = w0.put("b2f", [2 * NE, D], F32)
        bs2f = w0.put("bs2f", [2, D], F32)
        lowf = w0.put("lowf", [2 * NE, 2 * F], F32)
        gwf = w0.put("gwf", [P, KD, NE], F32)
        maski = w0.put("maski", [P, B, KV], I32)
        mfull = w0.put("mfull", [P, B, KV], F32)
        ints = w0.put("ints", [P, P], I32)
        gains_raw = w0.put("gains_raw", [P, 4], F32)
        assert w0.at <= w1.at

        c1 = Area(area_b, area_b2)
        ctxT = c1.put("ctxT", [P, B, KD, KV], F32)
        wk = c1.put("wk", [P, KD, DH], F32)
        wv = c1.put("wv", [P, KD, P], F32)
        wqT = c1.put("wqT", [DH, D], F32)
        wo = c1.put("wo", [P, KD, D], F32)
        bqk = c1.put("bqk", [DH, 2], F32)
        bvr = c1.put("bvr", [P, 1], F32)
        kT = c1.put("kT", [DH, B, KV], F32)
        vT = c1.put("vT", [P, B, KV], F32)
        kqT = c1.put("kqT", [P, KD, B, KV], F32)
        kbias = c1.put("kbias", [KV, B], F32)
        vo = c1.put("vo", [97, B, D], F32)
        zeros = c1.put("zeros", [P, D], F32)
        cnt_i = c1.put("cnt_i", [2 * NE, 2], I32)
        cnt_f = c1.put("cnt_f", [2 * NE, 4], F32)
        ge_in = c1.put("ge_in", [2 * NE, NT], F32)
        ge_ex = c1.put("ge_ex", [2 * NE, NT], F32)
        ones8 = c1.put("ones8", [NE, 1], F32)
        shift8 = c1.put("shift8", [NE, 1], F32)
        rank16 = c1.put("rank16", [P, 2 * NE], BF16)
        padpos = c1.put("padpos", [P, NE], U32)
        shifts = c1.put("shifts", [P, NE, NG * 2 * GT], F32)
        c2 = Area(area_b2, top)
        wint = c2.put("wint", [P, 9, 512], F32R)
        xg = [c2.put(f"xg{p}", [P, D], F32) for p in range(4)]
        yg = [c2.put(f"yg{p}", [P, D], F32) for p in range(4)]
        xTh = [c2.put(f"xTh{p}", [P, KD * P], F32R) for p in range(2)]
        xTl = [c2.put(f"xTl{p}", [P, KD * P], F32R) for p in range(2)]
        hid = [c2.put(f"hid{p}", [P, F], F32) for p in range(2)]
        hTh = [c2.put(f"hTh{p}", [P, KD * P], F32R) for p in range(2)]
        hTl = [c2.put(f"hTl{p}", [P, KD * P], F32R) for p in range(2)]
        sel = [c2.put(f"sel{p}", [2 * NE, P], F32R) for p in range(4)]
        wgv = wint[:, 0:3, :].rearrange("p a n -> p (a n)").rearrange("p (k n) -> p k n", k=KD)
        wuv = wint[:, 3:6, :].rearrange("p a n -> p (a n)").rearrange("p (k n) -> p k n", k=KD)
        wdv = wint[:, 6:9, :].rearrange("p a n -> p (a n)").rearrange("p (k n) -> p k n", k=ML)

        a3 = Area(area_a, area_b)
        xa = a3.put("xa", [P, GB, GT, D], F32)
        xf = a3.put("xf", [P, GB, GT, D], F32)
        ost = [a3.put(f"ost{c}", [P, GT, D], F32) for c in range(GB)]
        yr = a3.put("yr", [P, GB, 2, GT, D], F32)
        n3 = a3.put("n3", [P, GB, GT, D], F32)
        n3T = a3.put("n3T", [P, KD, GB, GT * P], F32)
        attnT = a3.put("attnT", [97, GB, GT * P], F32)
        n4 = a3.put("n4", [P, GT, D], F32)
        n4Th = [a3.put(f"n4Th{c}", [P, KD, GT * P], F32R) for c in range(GB)]
        n4Tl = [a3.put(f"n4Tl{c}", [P, KD, GT * P], F32R) for c in range(GB)]
        sl3 = [a3.put(f"sl3{p}", [P, 512], F32) for p in range(2)]
        g3h = a3.put("g3h", [P, ML, 512], F32R)
        g3l = a3.put("g3l", [P, ML, 512], F32R)
        kqb = a3.put("kqb", [P, KD, KV], F32)
        vob = a3.put("vob", [97, D], F32)
        vscale = a3.put("vscale", [97, 1], F32)
        smax2 = a3.put("smax2", [KV, GB], F32)
        smax = a3.put("smax", [KV, 1], F32)
        sbias = a3.put("sbias", [KV, 2], F32)
        ssum2 = a3.put("ssum2", [KV, GB], F32)
        ssum = a3.put("ssum", [KV, 1], F32)
        gpos = a3.put("gpos", [P, GB, 2, GT], U32)
        gw3 = a3.put("gw3", [P, GB, 2, GT], F32)
        st3 = [a3.put(f"st3{c}", [P, GB * GT, 6], F32) for c in range(2)]
        mv3 = [a3.put(f"mv3{c}", [P, GB * GT, 2], F32) for c in range(2)]
        ve3 = [a3.put(f"ve3{c}", [P, GB * GT], F32) for c in range(2)]
        rs3 = [a3.put(f"rs3{c}", [P, GB * GT], F32) for c in range(2)]

        bank = ctx.enter_context(nc.psum_tensor("bank", [P, 8, 512], F32))

        xs = nc.dram_tensor("rows_by_expert", [ROWS, D], F32, kind="Internal").ap()
        ys = nc.dram_tensor("expert_out", [NT * P, D], F32, kind="Internal").ap()
        xmid = nc.dram_tensor("x_shared", [T, D], F32, kind="Internal").ap()

        def rows(t, g, n=GT):
            return t[bass.ds(g * (GT * P), n * P), :].rearrange("(j p) d -> p j d", p=P)

        def above_zero(n):
            return not isinstance(n, int) or n > 0


        class Turn:

            def __init__(self, loop, every, c):
                self.loop, self.every, self.c = loop, every, c

            def __call__(self, k=0):
                return self.loop * self.every + (self.c + k)

            def before(self, k=0):
                return self.loop + (self.c + k) // self.every

            def slot(self, k=0):
                return (self.c + k) % self.every

        block = ctx.enter_context(nc.Block())

        @block.sync
        def _(sp):
            def small(dst, src, name="small_in"):
                sp.dma_start(dst, src).then_inc(sem(name), 16)

            def load_x(g, p):
                if above_zero(GT * (g - 1)):
                    sp.wait_ge(sem("x1_done"), GT * (g - 1)).then_inc(sem("passed"), 1)
                sp.dma_start(xin[p], rows(i["x"], g)).then_inc(sem(f"x_in{p}"), 16)

            def load_expert(e):
                for c in range(3):
                    sp.wait_ge(sem(f"low_done{c}"), e + 2).then_inc(sem("passed"), 1)
                    src = i["wexp"][bass.ds(e * (3 * P) + c * P, P), :]
                    sp.dma_start(stage[c], src).then_inc(sem(f"stage_in{c}"), 16)

            def store_mid(f, p):
                sp.wait_ge(sem("shared_done"), f + 1).then_inc(sem("passed"), 1)
                sp.dma_start(rows(xmid, f), x1[p]).then_inc(sem(f"mid_out{p}"), 16)

            load_x(0, 0)
            small(ctxTm.rearrange("p b k s -> p (b k s)"), i["ctx_cols"], "ctx_in")
            small(maski, i["mask"].partition_broadcast(P), "ctx_in")
            for c in range(3):
                sp.dma_start(stage[c], i["wsh"][c * P:(c + 1) * P, :]).then_inc(sem(f"stage_in{c}"), 16)
            small(ctxr, i["ctx"].rearrange("b s d -> s b d"), "ctxr_in")
            small(gains_raw[:, 0:2], i["g_xattn"].partition_broadcast(P))
            small(gains_raw[:, 2:4], i["g_ffn"].partition_broadcast(P))
            small(gbias, i["gate_b"].partition_broadcast(P))
            small(gwf.rearrange("p k e -> p (k e)"), i["gate_w"])
            small(bs13.rearrange("p a m -> p (a m)"), i["bs13"])
            small(bs2f, i["bs2"].partition_broadcast(2))
            for h in range(2):
                small(b13f[h * NE:(h + 1) * NE, :], i["b13"])
                small(b2f[h * NE:(h + 1) * NE, :], i["b2"])
            load_x(1, 1)
            for c in range(3):
                sp.wait_ge(sem(f"low_done{c}"), 1)
                sp.dma_start(stage[c], i["wsh"][(c + 3) * P:(c + 4) * P, :]).then_inc(sem(f"stage_in{c}"), 16)

            def step(g, p, load=True, store=True):
                load_expert(g)
                if load:
                    load_x(g + 2, p)
                if store:
                    store_mid(g - 1, 1 - p)

            step(0, 0, store=False)
            step(1, 1)
            with sp.Fori(0, 2) as it:
                step(it * 2 + 2, 0)
                step(it * 2 + 3, 1)
            step(6, 0, load=False)
            step(7, 1, load=False)
            sp.wait_ge(sem("t2_done"), NG)
            sp.wait_ge(sem("x1_done"), GT * NG)
            for c in range(3):
                sp.wait_ge(sem(f"low_done{c}"), NG + 2)
            for dst, src in ((ctxT.rearrange("p b k s -> p (b k s)"), "ctx_cols"), (wk.rearrange("p k j -> p (k j)"), "wk"),
                             (wv.rearrange("p k j -> p (k j)"), "wv"), (wqT, "wqT"), (wo.rearrange("p k j -> p (k j)"), "wo"),
                             (bqk, "bqk"), (bvr, "bv")):
                small(dst, i[src], "l1_in")
            for b in range(B):
                small(vo[96:97, b, :], i["bo"], "l1_in")
            sp.wait_ge(sem("filled"), 1)
            small(xs[SPARE:ROWS, :].rearrange("(a p) d -> p a d", p=P),
                  zeros.unsqueeze(1).broadcast_to([P, NE, D]), "spare_out")
            store_mid(7, 1)

            def load_tile(t, s):
                row = sp.value_load(tile_row[0:1, bass.ds(t, 1)], min_val=0, max_val=ROWS - P)
                if above_zero(t - 3):
                    sp.wait_ge(sem("tx_done"), t - 3).then_inc(sem("passed"), 1)
                sp.dma_start(xg[s], xs[bass.ds(row, P), :]).then_inc(sem(f"tile_in{s}"), 16)

            def store_tile(t, s):
                sp.wait_ge(sem("y_done"), t + 1).then_inc(sem("passed"), 1)
                sp.dma_start(ys[bass.ds(t * P, P), :], yg[s]).then_inc(sem(f"tile_out{s}"), 16)

            sp.wait_ge(sem("table_done"), 2)
            sp.wait_ge(sem("spare_out"), 16)
            for p in range(2):
                sp.wait_ge(sem(f"scattered{p}"), NG // 2 * 2 * GT * 16)
            sp.wait_ge(sem("pad_out"), 16 * NE)
            sp.wait_ge(sem("shared_done"), NG)
            for p in range(2):
                sp.wait_ge(sem(f"mid_out{p}"), 16 * (NG // 2))
            for t in range(4):
                load_tile(t, t)
            for t in range(4):
                load_tile(t + 4, t)
            with sp.Fori(0, NT // 4 - 2) as it:
                for r in range(4):
                    load_tile(it * 4 + 8 + r, r)
                    store_tile(it * 4 + r, r)
            for t in range(NT - 8, NT):
                store_tile(t, t % 4)

            def load_a(b):
                sp.dma_start(xa.rearrange("p c j d -> p (c j) d"), rows(xmid, b * GB, GB * GT)).then_inc(sem("xa_in"), 16)

            def store_out(b, c):
                sp.wait_ge(sem("out_done"), b * GB + c + 1).then_inc(sem("passed"), 1)
                sp.dma_start(rows(out, b * GB + c), ost[c]).then_inc(sem(f"out_out{c}"), 16)

            def step3(b):
                sp.wait_ge(sem("x3_done"), b * GB + 2).then_inc(sem("passed"), 1)
                load_a(b + 1)
                for c in range(GB):
                    store_out(b, c)

            sp.wait_ge(sem("y_mm_done"), NT)
            load_a(0)
            with sp.Fori(0, B - 1) as b:
                step3(b)
            for c in range(GB):
                store_out(B - 1, c)
            for c in range(GB):
                sp.wait_ge(sem(f"out_out{c}"), 16 * B)

        @block.gpsimd
        def _(pool):
            def chained(ins):
                pool_count[0] += 1
                ins.then_inc(sem("pool_const"), 1)
                pool.wait_ge(sem("pool_const"), pool_count[0])

            pool_count = [0]
            chained(pool.memset(ident, 0.0))
            chained(pool.affine_select(out=ident, in_=ident, compare_op=ALU.not_equal, fill=1.0, base=0,
                                       pattern=[[-1, P]], channel_multiplier=1))
            chained(pool.memset(halfpow, -0.5))
            chained(pool.memset(onesb, 1.0))
            chained(pool.memset(tri, 1.0))
            chained(pool.affine_select(out=tri, in_=tri, compare_op=ALU.is_gt, fill=0.0, base=0,
                                       pattern=[[1, P]], channel_multiplier=-1))
            for m, op in ((incl, ALU.is_ge), (excl, ALU.is_gt)):
                chained(pool.memset(m, 1.0))
                chained(pool.affine_select(out=m, in_=m, compare_op=op, fill=0.0, base=0,
                                           pattern=[[0, 2], [1, NE]], channel_multiplier=-1))
            for dst, pattern, mult, parts in ((expert_no, [[1, NE]], 0, P), (expert_row, [[RC, NE]], 0, P),
                                              (pad_row, [[RC, NE]], 1, P), (tile_no, [[1, NT]], 0, 2 * NE)):
                n = pattern[0][1]
                chained(pool.iota(ints[0:parts, 0:n], pattern, base=0, channel_multiplier=mult))
                chained(pool.tensor_copy(dst, ints[0:parts, 0:n]))

            def rstd_of(which, g, done):
                pool.wait_ge(sem(f"stats{which}"), g + 1).then_inc(sem("passed"), 1)
                pool.tensor_scalar(ve[which], mv[which][:, :, 1], EPS, None, ALU.add).then_inc(sem(f"var{which}"), 1)
                pool.wait_ge(sem(f"var{which}"), g + 1).then_inc(sem("passed"), 1)
                pool.tensor_tensor(rstd[which], ve[which], halfpow[:, 0:GT], ALU.pow).then_inc(sem(done), 1)

            def low_part(c, high, low, n):
                pool.wait_ge(sem(f"high_done{c}"), n).then_inc(sem("passed"), 1)
                pool.tensor_tensor(low, stage[c], high, ALU.subtract).then_inc(sem(f"low_done{c}"), 1)

            def expert_low(g, c):
                if c < 2:
                    high, low = (w[:, bass.ds(g * KD + c, 1), :].rearrange("p a n -> p (a n)") for w in (w13h, w13l))
                else:
                    high, low = (w[:, bass.ds(g, 1), :].rearrange("p a n -> p (a n)") for w in (w2h, w2l))
                low_part(c, high, low, g + 3)

            def hidden_low(f, m):
                pool.wait_ge(sem("hh_done"), MS * f + m + 1).then_inc(sem("passed"), 1)
                pool.tensor_tensor(hl[:, m, :], sil[m % 2], hh[:, m, :], ALU.subtract).then_inc(sem("hl_done"), 1)

            def scatter(f, p):
                pool.wait_ge(sem("pos_done"), f + 1).then_inc(sem("passed"), 1)
                for k in range(2):
                    for j in range(GT):
                        pool.indirect_dma_start(
                            out=xs, out_offset=bass.IndirectOffsetOnAxis(ap=pos[p][:, k, j:j + 1], axis=0),
                            in_=n2[p][:, j, :], in_offset=None).then_inc(sem(f"scattered{p}"), 16)

            def step(g, p, attn=True, ffn=True, nxt=True):
                f = g - 1
                if nxt:
                    rstd_of(0, g + 1, "rstd_a")
                if attn:
                    expert_low(g, 0)
                if ffn:
                    hidden_low(f, 0)
                if attn:
                    expert_low(g, 1)
                if ffn:
                    hidden_low(f, 1)
                if attn:
                    rstd_of(1, g, "rstd_b")
                    expert_low(g, 2)
                if ffn:
                    hidden_low(f, 2)
                    hidden_low(f, 3)
                    scatter(f, 1 - p)

            rstd_of(0, 0, "rstd_a")
            for r in range(2):
                for c in range(3):
                    low_part(c, wsh[:, 3 * r + c, :], wsl[:, 3 * r + c, :], r + 1)
            step(0, 0, ffn=False)
            step(1, 1)
            step(2, 0)
            with pool.Fori(0, 2) as it:
                step(it * 2 + 3, 1)
                step(it * 2 + 4, 0)
            step(7, 1, nxt=False)
            pool.wait_ge(sem("t2_done"), NG)
            pool.wait_ge(sem("x1_done"), GT * NG)
            pool.memset(zeros, 0.0).then_inc(sem("filled"), 1)
            pool.memset(ones8, 1.0).then_inc(sem("filled"), 1)
            pool.wait_ge(sem("filled"), 2)
            pool.memset(vo[64:96, :, :], 0.0).then_inc(sem("filled"), 1)
            pool.wait_ge(sem("filled"), 3)
            step(8, 0, attn=False, nxt=False)
            pool.wait_ge(sem("padpos_done"), 1)
            for e in range(NE):
                pool.indirect_dma_start(out=xs, out_offset=bass.IndirectOffsetOnAxis(ap=padpos[:, e:e + 1], axis=0),
                                        in_=zeros, in_offset=None).then_inc(sem("pad_out"), 16)
            pool.wait_ge(sem("shared_done"), NG)
            pool.wait_ge(sem("d_done"), NG)
            for p in range(2):
                pool.wait_ge(sem(f"scattered{p}"), NG // 2 * 2 * GT * 16)
                pool.wait_ge(sem(f"mid_out{p}"), 16 * (NG // 2))
            for c in range(3):
                pool.dma_start(wint[:, 3 * c:3 * c + 3, :], i["wint"][3 * c:3 * c + 3].rearrange("c p n -> p c n"))\
                    .then_inc(sem("wint_in"), 16)

            pool.wait_ge(sem("route_kept"), 3 * NG)
            pool.wait_ge(sem("row_shift_done"), 1)
            flat = [t.rearrange("p g k j -> p (g k j)") for t in (expert_all, pos_all, out_row)]
            for e in range(NE):
                pool.tensor_scalar(shifts[:, e, :], flat[0], float(e), row_shift[:, e:e + 1], ALU.is_equal, ALU.mult)\
                    .then_inc(sem("shifts_done"), 1)
            pool.wait_ge(sem("shifts_done"), NE)
            for n in (4, 2, 1):
                pool.tensor_tensor(shifts[:, 0:n, :], shifts[:, 0:n, :], shifts[:, n:2 * n, :], ALU.add)\
                    .then_inc(sem("shifts_done"), n)
                pool.wait_ge(sem("shifts_done"), NE + 8 - n)
            pool.tensor_tensor(shifts[:, 1, :], flat[1], shifts[:, 0, :], ALU.add).then_inc(sem("shifts_done"), 1)
            pool.wait_ge(sem("shifts_done"), 2 * NE)
            pool.tensor_copy(flat[2], shifts[:, 1, :]).then_inc(sem("shifts_done"), 1)
            pool.wait_ge(sem("shifts_done"), 2 * NE + 1)

            def gather(b, part):
                c, k = part // 2, part % 2
                for j in range(GT):
                    pool.indirect_dma_start(
                        out=yr[:, c, k, j, :], out_offset=None, in_=ys,
                        in_offset=bass.IndirectOffsetOnAxis(ap=gpos[:, c, k, j:j + 1], axis=0))\
                        .then_inc(sem("gathered"), 16)

            def gather_index(b):
                if above_zero(GB * GT * b):
                    pool.wait_ge(sem("x2b_done"), GB * GT * b).then_inc(sem("passed"), 1)
                if not isinstance(b, int) or b:
                    pool.wait_ge(sem("gathered"), 256 * b).then_inc(sem("passed"), 1)
                pool.tensor_copy(gpos, out_row[:, bass.ds(b * GB, GB), :, :]).then_inc(sem("gpos_done"), 1)
                pool.wait_ge(sem("gpos_done"), b + 1).then_inc(sem("passed"), 1)

            def rstd3(which, lo, n, count):
                pool.wait_ge(sem(f"stats3{which}"), count).then_inc(sem("passed"), 1)
                pool.tensor_scalar(ve3[which][:, lo:lo + n], mv3[which][:, lo:lo + n, 1], EPS, None, ALU.add)\
                    .then_inc(sem(f"var3{which}"), 1)
                pool.wait_ge(sem(f"var3{which}"), count).then_inc(sem("passed"), 1)
                pool.tensor_tensor(rs3[which][:, lo:lo + n], ve3[which][:, lo:lo + n], halfpow[:, 0:n], ALU.pow)\
                    .then_inc(sem(f"rs3{which}"), 1)

            def low3(b, c, m):
                pool.wait_ge(sem("g3h_done"), (b * GB + c) * ML + m + 1).then_inc(sem("passed"), 1)
                pool.tensor_tensor(g3l[:, m, :], sl3[m % 2], g3h[:, m, :], ALU.subtract).then_inc(sem("g3l_done"), 1)

            pool.wait_ge(sem("y_mm_done"), NT)
            pool.wait_ge(sem("y_done"), NT)
            for s in range(4):
                pool.wait_ge(sem(f"tile_out{s}"), 16 * (NT // 4))
            gather_index(0)
            for q in range(4):
                gather(0, q)
            pool.wait_ge(sem("gathered"), 256)
            pool.memset(attnT[64:96, :, :], 0.0).then_inc(sem("attn_pad"), 1)
            pool.wait_ge(sem("attn_pad"), 1)
            pool.memset(attnT[96:97, :, :], 1.0).then_inc(sem("attn_pad"), 1)
            pool.wait_ge(sem("attn_pad"), 2)
            rstd3(0, 0, GB * GT, 1)
            gather_index(1)
            for q in range(4):
                gather(1, q)
            rstd3(1, 0, GT, 1)

            def first_half(b, last=False):
                rstd3(1, GT, GT, b * GB + 2)
                for m in range(ML):
                    low3(b, 0, m)
                if not last:
                    rstd3(0, 0, GB * GT, b + 2)

            def second_half(b, more):
                for m in range(3):
                    low3(b, 1, m)
                    if more and m == 1:
                        gather_index(b + 2)
                rstd3(1, 0, GT, b * GB + 3)
                for m in range(3, ML):
                    low3(b, 1, m)
                if more:
                    for q in range(4):
                        gather(b + 2, q)

            with pool.Fori(0, B - 2) as b:
                first_half(b)
                second_half(b, True)
            first_half(B - 2)
            second_half(B - 2, False)
            first_half(B - 1, last=True)
            for m in range(ML):
                low3(B - 1, 1, m)

        @block.scalar
        def _(act):
            def copy(dst, src):
                return act.activation(dst, src, ACT.Copy)

            def stage_high(c, dst, n):
                act.wait_ge(sem(f"stage_in{c}"), 16 * n).then_inc(sem("passed"), 1)
                copy(dst, stage[c]).then_inc(sem(f"high_done{c}"), 1)

            def expert_high(g, c):
                if c < 2:
                    high = w13h[:, bass.ds(g * KD + c, 1), :].rearrange("p a n -> p (a n)")
                else:
                    high = w2h[:, bass.ds(g, 1), :].rearrange("p a n -> p (a n)")
                stage_high(c, high, g + 3)

            def t1_copy(g):
                if above_zero(g):
                    act.wait_ge(sem("s_done"), g)
                for k in range(KD):
                    act.wait_ge(sem("t1_done"), KD * g + k + 1)
                    copy(n1T[:, k, :], bank[:, 4 + k, :]).then_inc(sem("n1T_done"), 1)

            def softmax(g):
                act.wait_ge(sem("negmax_done"), g + 1)
                if above_zero(g):
                    act.wait_ge(sem("pt_done"), g)
                if above_zero(2 * g):
                    act.wait_ge(sem("pscale_done"), 2 * g)
                for j in range(GT):
                    act.activation(probs[:, j, :], bank[:, 6, j * P:j * P + KV], ACT.Exp, bias=negmax[:, j:j + 1],
                                   accum_out=psums[:, j:j + 1]).then_inc(sem("probs_done"), 1)

            def pt_copy(g):
                if above_zero(GT * g):
                    act.wait_ge(sem("pv_done"), GT * g)
                act.wait_ge(sem("pt_done"), g + 1)
                copy(probsT, bank[0:KV, 7, :]).then_inc(sem("probsT_done"), 1)

            def silu(f, m):
                act.wait_ge(sem("u_done"), MS * f + m + 1)
                if above_zero(MS * f + m - 1):
                    act.wait_ge(sem("hl_done"), MS * f + m - 1)
                act.activation(sil[m % 2], bank[:, 2 * (m % 2), :], ACT.Silu, bias=bs13[:, 0, m:m + 1])\
                    .then_inc(sem("silu_done"), 1)

            def hidden_high(f, m):
                act.wait_ge(sem("h_done"), MS * f + m + 1)
                if above_zero(f):
                    act.wait_ge(sem("d_done"), f)
                copy(hh[:, m, :], sil[m % 2]).then_inc(sem("hh_done"), 1)

            def t2_copy(g):
                act.wait_ge(sem("t2_done"), g + 1)
                for k in range(KD):
                    copy(n2Th[:, k, :], bank[:, 4 + k, :]).then_inc(sem("n2Th_done"), 1)

            def step(g, p, attn=True, ffn=True, nxt=True):
                f = g - 1
                if attn:
                    softmax(g)
                if ffn:
                    act.wait_ge(sem("dlog_done"), f + 1)
                    act.activation(elog, dlog, ACT.Exp).then_inc(sem("elog_done"), 1)
                if attn:
                    expert_high(g, 0)
                if ffn:
                    silu(f, 0)
                if attn:
                    pt_copy(g)
                if ffn:
                    hidden_high(f, 0)
                if attn:
                    expert_high(g, 1)
                if ffn:
                    for m in range(1, MS):
                        silu(f, m)
                        hidden_high(f, m)
                if nxt:
                    t1_copy(g + 1)
                if attn:
                    expert_high(g, 2)
                    t2_copy(g)

            act.wait_ge(sem("small_in"), 16 * 10)
            act.activation(gains, gains_raw, ACT.Tanh).then_inc(sem("gains_done"), 1)
            for c in range(3):
                stage_high(c, wsh[:, c, :], 1)
            t1_copy(0)
            for c in range(3):
                stage_high(c, wsh[:, 3 + c, :], 2)
            step(0, 0, ffn=False)
            step(1, 1)
            step(2, 0)
            with act.Fori(0, 2) as it:
                step(it * 2 + 3, 1)
                step(it * 2 + 4, 0)
            step(7, 1, nxt=False)
            step(8, 0, attn=False, nxt=False)

            act.wait_ge(sem("kv_mm"), 1)
            act.activation(kT.rearrange("j b s -> j (b s)"), bank[0:DH, 4, 0:B * KV], ACT.Identity, bias=bqk[:, 1:2])\
                .then_inc(sem("kT_done"), 1)
            act.activation(vT.rearrange("j b s -> j (b s)"), bank[:, 5, 0:B * KV], ACT.Identity, bias=bvr)\
                .then_inc(sem("kT_done"), 1)
            act.wait_ge(sem("kq_mm"), 1)
            for m in range(KD):
                copy(kqT[:, m, :, :].rearrange("p b s -> p (b s)"), bank[:, 6 * m, 0:B * KV]).then_inc(sem("kq_done"), 1)
            copy(kbias, bank[0:KV, 4, 0:B]).then_inc(sem("kq_done"), 1)
            act.wait_ge(sem("vo_mm"), 1)
            act.wait_ge(sem("filled"), 3)
            for h in range(2):
                copy(vo[0:KV, 2 * h:2 * h + 2, :].rearrange("p b d -> p (b d)"), bank[0:KV, 2 + h, :])\
                    .then_inc(sem("vo_done"), 1)

            def step2(t, x=True, h=True, th=True, y=True):
                p = t.slot() % 2
                if h:
                    act.wait_ge(sem("hm_done"), t(1))
                    if above_zero(t(-1)):
                        act.wait_ge(sem("th_done"), t(-1))
                    act.activation(hid[p], bank[:, p, 0:F], ACT.Silu).then_inc(sem("silu2_done"), 1)
                if x:
                    act.wait_ge(sem("tx_done"), t(3))
                    copy(xTh[p], bank[:, 4 + p, 0:KD * P]).then_inc(sem("xTh_done"), 1)
                if th:
                    act.wait_ge(sem("th_done"), t())
                    copy(hTh[1 - p], bank[:, 3 - p, 0:KD * P]).then_inc(sem("hTh_done"), 1)
                if y:
                    s = t.slot(-2)
                    if above_zero(t.before(-2) * 16):
                        act.wait_ge(sem(f"tile_out{s}"), t.before(-2) * 16)
                    act.wait_ge(sem("y_mm_done"), t(-1))
                    copy(yg[s], bank[:, 6 + p, 0:D]).then_inc(sem("y_done"), 1)

            step2(Turn(0, 4, -2), h=False, th=False, y=False)
            step2(Turn(0, 4, -1), h=False, th=False, y=False)
            step2(Turn(0, 4, 0), th=False, y=False)
            step2(Turn(0, 4, 1), y=False)
            for c in range(2, 6):
                step2(Turn(0, 4, c))
            with act.Fori(0, (NT - 8) // 4) as it:
                for c in range(6, 10):
                    step2(Turn(it, 4, c))
            step2(Turn(0, 4, NT - 2), x=False)
            step2(Turn(0, 4, NT - 1), x=False)
            step2(Turn(0, 4, NT), x=False, h=False)
            step2(Turn(0, 4, NT + 1), x=False, h=False, th=False)

            def copy_n3(b):
                for c in range(GB):
                    for k in range(KD):
                        act.wait_ge(sem("t3_done"), (b * GB + c) * KD + k + 1)
                        copy(n3T[:, k, c, :], bank[:, 4 + 2 * c + k, :]).then_inc(sem("n3T_done"), 1)

            def softmax3(b):
                act.wait_ge(sem("sbias_done"), b + 1)
                if above_zero(b * GB * GT):
                    act.wait_ge(sem("o_done"), b * GB * GT)
                for c in range(GB):
                    act.activation(attnT[0:KV, c, :], bank[0:KV, 4 + c, :], ACT.Exp, scale=0.25, bias=sbias[:, 1:2],
                                   accum_out=ssum2[:, c:c + 1]).then_inc(sem("attn_done"), 1)

            def copy_n4(b, c):
                act.wait_ge(sem("t4_done"), b * GB + c + 1)
                base = 6 - 2 * c
                for k in range(KD):
                    copy(n4Th[c][:, k, :], bank[:, base + k, :]).then_inc(sem("n4Th_done"), 1)

            def hidden3(b, c, m):
                n = (b * GB + c) * ML + m
                act.wait_ge(sem("u3_done"), n + 1)
                if above_zero(n - 1):
                    act.wait_ge(sem("g3l_done"), n - 1)
                act.activation(sl3[m % 2], bank[:, 2 * (m % 2), :], ACT.Silu, scale=DEQ).then_inc(sem("sl3_done"), 1)
                act.wait_ge(sem("g3_done"), n + 1)
                if above_zero(b * GB + c):
                    act.wait_ge(sem("d3_done"), b * GB + c)
                copy(g3h[:, m, :], sl3[m % 2]).then_inc(sem("g3h_done"), 1)

            def step3(b, nxt=True):
                for m in range(3):
                    hidden3(b, 0, m)
                copy_n4(b, 1)
                for m in range(3, ML):
                    hidden3(b, 0, m)
                if nxt:
                    copy_n3(b + 1)
                hidden3(b, 1, 0)
                hidden3(b, 1, 1)
                if nxt:
                    softmax3(b + 1)
                for m in range(2, ML):
                    hidden3(b, 1, m)
                if nxt:
                    copy_n4(b + 1, 0)

            act.wait_ge(sem("y_mm_done"), NT)
            copy_n3(0)
            act.wait_ge(sem("attn_pad"), 2)
            softmax3(0)
            copy_n4(0, 0)
            step3(0)
            with act.Fori(1, B - 1) as b:
                step3(b)
            step3(B - 1, nxt=False)

        @block.tensor
        def _(pe):
            mm = pe.matmul

            def t1(g, rows_in):
                pe.wait_ge(sem("n1_done"), GT * (g + 1))
                if above_zero(GT * g):
                    pe.wait_ge(sem("x1_done"), GT * g)
                if above_zero(KD * (g - 1)):
                    pe.wait_ge(sem("n2Tl_done"), KD * (g - 1))
                for k in range(KD):
                    for j in range(GT):
                        last = pe.transpose(bank[:, 4 + k, j * P:(j + 1) * P], rows_in[:, j, k * P:(k + 1) * P], ident)
                    last.then_inc(sem("t1_done"), 1)

            def scores(g, b):
                pe.wait_ge(sem("n1T_done"), KD * (g + 1))
                if above_zero(GT * g):
                    pe.wait_ge(sem("probs_done"), GT * g)
                for j in range(GT):
                    o = bank[:, 6, j * P:j * P + KV]
                    for k in range(KD):
                        mm(o, n1T[:, k, j * P:(j + 1) * P], at(ctxTm, b, k), start=(k == 0), stop=False)
                    last = mm(o, onesf, negrow[0:1, bass.ds(b, 1), :].rearrange("p a s -> p (a s)"), start=False, stop=True)
                last.then_inc(sem("s_done"), 1)

            def at(t, b, k):
                return t[:, bass.ds(b, 1), k, :].rearrange("p a s -> p (a s)")

            def probs_t(g):
                pe.wait_ge(sem("probs_done"), GT * (g + 1))
                if above_zero(g):
                    pe.wait_ge(sem("logit_done"), g)
                for j in range(GT):
                    last = pe.transpose(bank[0:KV, 7, j * P:(j + 1) * P], probs[:, j, :], ident)
                last.then_inc(sem("pt_done"), 1)

            def values(g, b):
                pe.wait_ge(sem("probsT_done"), g + 1)
                if above_zero(KD * g):
                    pe.wait_ge(sem("n2Tl_done"), KD * g)
                for j in range(GT):
                    mm(bank[:, 4 + j // 2, (j % 2) * D:(j % 2 + 1) * D], probsT[:, j * P:(j + 1) * P],
                       ctxr[:, bass.ds(b, 1), :].rearrange("s a d -> s (a d)"), start=True, stop=True).then_inc(sem("pv_done"), 1)

            def t2(g, p, nxt):
                pe.wait_ge(sem("n2_done"), GT * (g + 1))
                pe.wait_ge(sem("n1T_done"), KD * (g + 2 if nxt else g + 1))
                pe.wait_ge(sem("x1_done"), GT * (g + 1))
                for k in range(KD):
                    for j in range(GT):
                        last = pe.transpose(bank[:, 4 + k, j * P:(j + 1) * P], n2[p][:, j, k * P:(k + 1) * P], ident)
                last.then_inc(sem("t2_done"), 1)

            def three(o, ah, al, bh, bl, first, final):
                mm(o, ah, bh, start=first, stop=False)
                mm(o, ah, bl, start=False, stop=False)
                return mm(o, al, bh, start=False, stop=final)

            def up(f, m):
                if m < 2:
                    if above_zero(f):
                        pe.wait_ge(sem("shared_done"), f)
                    if m == 0:
                        pe.wait_ge(sem("n2Tl_done"), KD * (f + 1))
                        pe.wait_ge(sem("n2Th_done"), KD * (f + 1))
                else:
                    pe.wait_ge(sem("h_done"), MS * f + m - 1)
                for w in range(2):
                    o = bank[:, 2 * (m % 2) + w, :]
                    for k in range(KD):
                        c = KD * w + k
                        s = slice(m * P, (m + 1) * P)
                        last = three(o, wsh[:, c, s], wsl[:, c, s], n2Th[:, k, :], n2Tl[:, k, :], k == 0, k == KD - 1)
                last.then_inc(sem("u_done"), 1)

            def down(f, ks):
                for k in ks:
                    if k == 0:
                        pe.wait_ge(sem("h_done"), MS * f + MS)
                    pe.wait_ge(sem("hh_done"), MS * f + k + 1)
                    pe.wait_ge(sem("hl_done"), MS * f + k + 1)
                    c, s = 4 + k // 2, slice((k % 2) * D, (k % 2 + 1) * D)
                    for j in range(GT):
                        t = slice(j * P, (j + 1) * P)
                        o = bank[:, j, 0:D]
                        if k == 0:
                            mm(o, ones2, bs2, start=True, stop=False)
                        last = three(o, hh[:, k, t], hl[:, k, t], wsh[:, c, s], wsl[:, c, s], False, k == MS - 1)
                if ks[-1] == MS - 1:
                    last.then_inc(sem("d_done"), 1)

            def gate(g):
                pe.wait_ge(sem("n2Tl_done"), KD * (g + 1))
                pe.wait_ge(sem("n2Th_done"), KD * (g + 1))
                pe.wait_ge(sem("probsT_done"), g + 1)
                if above_zero(g):
                    pe.wait_ge(sem("rrow_done"), g)
                for j in range(GT):
                    t = slice(j * P, (j + 1) * P)
                    for k in range(KD):
                        last = three(bank[:, 7, j * NE:(j + 1) * NE], n2Th[:, k, t], n2Tl[:, k, t], gwh[:, k, :], gwl[:, k, :],
                                     k == 0, k == KD - 1)
                last.then_inc(sem("gate_done"), 1)

            def rank(f):
                pe.wait_ge(sem("routed_done"), f + 1)
                pe.wait_ge(sem("base_done"), f + 1)
                o = bank[:, 7, 0:GT * NE].rearrange("p (j e) -> p j e", j=GT)
                mm(o, tri, routed, start=True, stop=False)
                for j in range(GT - 1):
                    mm(o[:, j + 1:GT, :], onesb, routed[:, j:j + 1, :].broadcast_to([P, GT - 1 - j, NE]),
                       start=False, stop=False, skip_group_check=True)
                mm(o, onesb, rank_base.unsqueeze(1).broadcast_to([P, GT, NE]), start=False, stop=True).then_inc(sem("rank_done"), 1)

            def step(g, b, bn, p, attn=True, ffn=True, nxt=True):
                f = g - 1
                if ffn:
                    up(f, 0)
                if attn:
                    probs_t(g)
                if ffn:
                    up(f, 1)
                if attn:
                    values(g, b)
                if ffn:
                    up(f, 2)
                    if attn:
                        pe.wait_ge(sem("probsT_done"), g + 1)
                    rank(f)
                    up(f, 3)
                if nxt:
                    t1(g + 1, n1)
                if ffn:
                    down(f, (0, 1))
                if attn:
                    t2(g, p, nxt)
                if ffn:
                    down(f, (2, 3))
                if attn:
                    gate(g)
                if nxt:
                    scores(g + 1, bn)

            pe.wait_ge(sem("pool_const"), 18)
            t1(0, n1)
            pe.wait_ge(sem("ctx_ready"), 3)
            scores(0, 0)
            pe.wait_ge(sem("ctxr_in"), 16)
            step(0, 0, 0, 0, ffn=False)
            for c in range(3):
                pe.wait_ge(sem(f"low_done{c}"), 2)
            pe.wait_ge(sem("bias_ready"), 4)
            step(1, 0, 1, 1)
            step(2, 1, 1, 0)
            with pe.Fori(0, 2) as it:
                step(it * 2 + 3, it + 1, it + 2, 1)
                step(it * 2 + 4, it + 2, it + 2, 0)
            step(7, 3, 3, 1, nxt=False)
            f = NG - 1
            up(f, 0)
            up(f, 1)
            rank(f)
            up(f, 2)
            pe.wait_ge(sem("base_done"), NG + 1)
            pe.wait_ge(sem("rank16_done"), 2)
            mm(bank[0:2 * NE, 7, 0:1], rank16, onesb[:, 0:1], start=True, stop=True)
            mm(bank[:, 7, 8:8 + NE], onesb, rank_base, start=True, stop=True).then_inc(sem("count_mm"), 1)
            up(f, 3)
            pe.wait_ge(sem("tiles_done"), 1)
            pe.wait_ge(sem("padpos_done"), 1)
            mm(bank[0:2 * NE, 7, 0:1], incl.rearrange("p a e -> p (a e)"), cnt_f[0:NE, 0:1], start=True, stop=True)
            mm(bank[0:2 * NE, 7, 1:2], excl.rearrange("p a e -> p (a e)"), cnt_f[0:NE, 0:1], start=True, stop=True)
            mm(bank[:, 7, 16:16 + NE], cnt_f[0:NE, 0:1].broadcast_to([NE, P]), excl[:, 0, :], start=True, stop=True)\
                .then_inc(sem("count_mm"), 1)
            down(f, (0, 1))
            pe.wait_ge(sem("ge_done"), 3)
            pe.wait_ge(sem("filled"), 2)
            mm(bank[0:1, 7, 0:NT], ones8, ge_in[0:NE, :], start=True, stop=True)
            mm(bank[0:1, 7, 128:128 + NT], shift8, ge_in[0:NE, :], start=True, stop=True).then_inc(sem("count_mm"), 1)
            down(f, (2, 3))

            pe.wait_ge(sem("l1_in"), 16 * 11)
            pe.wait_ge(sem("n2Tl_done"), KD * NG)
            for k in range(KD):
                mm(bank[0:DH, 4, 0:B * KV], wk[:, k, :], ctxT[:, :, k, :], start=(k == 0), stop=(k == KD - 1))
            for k in range(KD):
                last = mm(bank[:, 5, 0:B * KV], wv[:, k, :], ctxT[:, :, k, :], start=(k == 0), stop=(k == KD - 1))
            last.then_inc(sem("kv_mm"), 1)
            pe.wait_ge(sem("kT_done"), 2)
            pe.wait_ge(sem("shared_done"), NG)
            for m in range(KD):
                mm(bank[:, 6 * m, 0:B * KV], wqT[:, m * P:(m + 1) * P], kT.rearrange("j b s -> j (b s)"), start=True, stop=True)
            for b in range(B):
                last = mm(bank[0:KV, 4, b:b + 1], kT[:, b, :], bqk[:, 0:1], start=True, stop=True)
            last.then_inc(sem("kq_mm"), 1)
            for b in range(B):
                o = bank[0:KV, 2 + b // 2, (b % 2) * D:(b % 2 + 1) * D]
                for k in range(KD):
                    last = mm(o, vT[:, b, :], wo[:, k, :], start=(k == 0), stop=(k == KD - 1))
            last.then_inc(sem("vo_mm"), 1)
            pe.wait_ge(sem("vo_done"), 2)
            pe.wait_ge(sem("kq_done"), 3)

            def tx(t, q, turns):
                pe.wait_ge(sem(f"tile_in{q}"), turns * 16)
                if above_zero(t - 1):
                    pe.wait_ge(sem("xTl_done"), t - 1)
                for k in range(KD):
                    last = pe.transpose(bank[:, 4 + q % 2, k * P:(k + 1) * P], xg[q][:, k * P:(k + 1) * P], ident)
                last.then_inc(sem("tx_done"), 1)

            def th(t, q):
                p = q % 2
                pe.wait_ge(sem("hid_done"), t + 1)
                if above_zero(t - 1):
                    pe.wait_ge(sem("hTl_done"), t - 1)
                for k in range(KD):
                    last = pe.transpose(bank[:, 2 + p, k * P:(k + 1) * P], hid[p][:, k * P:(k + 1) * P], ident)
                last.then_inc(sem("th_done"), 1)

            def hidden(t, q, e):
                p = q % 2
                pe.wait_ge(sem("xTl_done"), t + 1)
                if above_zero(t - 1):
                    pe.wait_ge(sem("hid_done"), t - 1)
                pe.wait_ge(sem("sel_done"), t + 1)
                mm(bank[:, p, :], sel[q], b13, start=True, stop=False)
                for k in range(KD):
                    wh, wl = (w[:, bass.ds(e * KD + k, 1), :].rearrange("p a n -> p (a n)") for w in (w13h, w13l))
                    s = slice(k * P, (k + 1) * P)
                    last = three(bank[:, p, :], xTh[p][:, s], xTl[p][:, s], wh, wl, False, k == KD - 1)
                last.then_inc(sem("hm_done"), 1)

            def outp(t, q, e):
                p = q % 2
                pe.wait_ge(sem("hTl_done"), t + 1)
                if above_zero(t - 1):
                    pe.wait_ge(sem("y_done"), t - 1)
                mm(bank[:, 6 + p, 0:D], sel[q], b2, start=True, stop=False)
                for k in range(KD):
                    wh, wl = (w[:, bass.ds(e, 1), k * D:(k + 1) * D].rearrange("p a n -> p (a n)") for w in (w2h, w2l))
                    s = slice(k * P, (k + 1) * P)
                    last = three(bank[:, 6 + p, 0:D], hTh[p][:, s], hTl[p][:, s], wh, wl, False, k == KD - 1)
                last.then_inc(sem("y_mm_done"), 1)

            def expert_of(t):
                return pe.value_load(tile_expert[0:1, bass.ds(t, 1)], min_val=0, max_val=NE - 1)

            def step2(t, x=True, h=True, hd=True, y=True):
                if h:
                    hidden(t(), t.slot(), expert_of(t()))
                if x:
                    tx(t(2), t.slot(2), t.before(2) + 1)
                if y:
                    outp(t(-2), t.slot(-2), expert_of(t(-2)))
                if hd:
                    th(t(-1), t.slot(-1))

            pe.wait_ge(sem("table_done"), 2)
            step2(Turn(0, 4, -2), h=False, hd=False, y=False)
            step2(Turn(0, 4, -1), h=False, hd=False, y=False)
            step2(Turn(0, 4, 0), hd=False, y=False)
            step2(Turn(0, 4, 1), y=False)
            for c in range(2, 6):
                step2(Turn(0, 4, c))
            with pe.Fori(0, (NT - 8) // 4) as it:
                for c in range(6, 10):
                    step2(Turn(it, 4, c))
            step2(Turn(0, 4, NT - 2), x=False)
            step2(Turn(0, 4, NT - 1), x=False)
            step2(Turn(0, 4, NT), x=False, h=False)
            step2(Turn(0, 4, NT + 1), x=False, h=False, hd=False)

            def t3(b):
                pe.wait_ge(sem("n3_done"), GB * GT * (b + 1))
                if above_zero(KD * GB * b):
                    pe.wait_ge(sem("n4Tl_done"), KD * GB * b)
                for c in range(GB):
                    for k in range(KD):
                        for j in range(GT):
                            last = pe.transpose(bank[:, 4 + 2 * c + k, j * P:(j + 1) * P], n3[:, c, j, k * P:(k + 1) * P], ident)
                        last.then_inc(sem("t3_done"), 1)

            def scores3(b):
                pe.wait_ge(sem("n3T_done"), GB * KD * (b + 1))
                pe.wait_ge(sem("kqb_done"), b + 1)
                for c in range(GB):
                    for k in range(KD):
                        last = mm(bank[0:KV, 4 + c, :], kqb[:, k, :], n3T[:, k, c, :], start=(k == 0), stop=(k == KD - 1))
                    last.then_inc(sem("s3_done"), 1)

            def out3(b):
                pe.wait_ge(sem("vob_done"), b + 1)
                pe.wait_ge(sem("attn_done"), GB * (b + 1))
                for c in range(GB):
                    base = 6 - 2 * c
                    for j in range(GT):
                        mm(bank[:, base + j // 2, (j % 2) * D:(j % 2 + 1) * D], attnT[:, c, j * P:(j + 1) * P], vob,
                           start=True, stop=True).then_inc(sem("o_done"), 1)

            def t4(b, c):
                pe.wait_ge(sem("n4_done"), GT * (b * GB + c + 1))
                pe.wait_ge(sem("x3_done"), b * GB + c + 1)
                base = 6 - 2 * c
                for k in range(KD):
                    for j in range(GT):
                        last = pe.transpose(bank[:, base + k, j * P:(j + 1) * P], n4[:, j, k * P:(k + 1) * P], ident)
                last.then_inc(sem("t4_done"), 1)

            def up3(b, c, m):
                n = (b * GB + c) * ML + m
                if m < 2:
                    if above_zero(b * GB + c):
                        pe.wait_ge(sem("out_done"), b * GB + c)
                    if m == 0:
                        pe.wait_ge(sem("n4Tl_done"), KD * (b * GB + c + 1))
                        pe.wait_ge(sem("n4Th_done"), KD * (b * GB + c + 1))
                else:
                    pe.wait_ge(sem("g3_done"), n - 1)
                for w, wt in enumerate((wgv, wuv)):
                    o = bank[:, 2 * (m % 2) + w, :]
                    for k in range(KD):
                        s = wt[:, k, m * P:(m + 1) * P]
                        mm(o, s, n4Th[c][:, k, :], start=(k == 0), stop=False)
                        last = mm(o, s, n4Tl[c][:, k, :], start=False, stop=(k == KD - 1))
                last.then_inc(sem("u3_done"), 1)

            def down3(b, c, ks):
                n = (b * GB + c) * ML
                for k in ks:
                    if k == 0:
                        pe.wait_ge(sem("g3_done"), n + ML)
                    pe.wait_ge(sem("g3h_done"), n + k + 1)
                    pe.wait_ge(sem("g3l_done"), n + k + 1)
                    for j in range(GT):
                        t = slice(j * P, (j + 1) * P)
                        mm(bank[:, j, 0:D], g3h[:, k, t], wdv[:, k, :], start=(k == 0), stop=False)
                        last = mm(bank[:, j, 0:D], g3l[:, k, t], wdv[:, k, :], start=False, stop=(k == ML - 1))
                if ks[-1] == ML - 1:
                    last.then_inc(sem("d3_done"), 1)

            def step3(b, nxt=True):
                for m in range(3):
                    up3(b, 0, m)
                t4(b, 1)
                for m in range(3, ML):
                    up3(b, 0, m)
                down3(b, 0, range(ML))
                if nxt:
                    t3(b + 1)
                up3(b, 1, 0)
                up3(b, 1, 1)
                if nxt:
                    scores3(b + 1)
                up3(b, 1, 2)
                up3(b, 1, 3)
                if nxt:
                    out3(b + 1)
                up3(b, 1, 4)
                up3(b, 1, 5)
                down3(b, 1, range(3))
                if nxt:
                    t4(b + 1, 0)
                down3(b, 1, range(3, ML))

            pe.wait_ge(sem("attn_pad"), 2)
            t3(0)
            scores3(0)
            out3(0)
            t4(0, 0)
            pe.wait_ge(sem("wint_in"), 48)
            step3(0)
            with pe.Fori(1, B - 1) as b:
                step3(b)
            step3(B - 1, nxt=False)

        @block.vector
        def _(dve):
            tt, ts, stt, cp = dve.tensor_tensor, dve.tensor_scalar, dve.scalar_tensor_tensor, dve.tensor_copy
            count = [0]

            def chained(ins):
                count[0] += 1
                ins.then_inc(sem("dve_const"), 1)
                dve.wait_ge(sem("dve_const"), count[0])

            chained(dve.memset(onesf, 1.0))
            chained(dve.memset(ones2.bitcast(F32), 1.0))
            for m, h in ((upper16, NE), (upper2, 1)):
                chained(dve.memset(m[:, 0:1], 0.0))
                chained(dve.memset(m[:, 1:2], 1.0))
                chained(dve.memset(m[0:h, 0:1], 1.0))
                chained(dve.memset(m[0:h, 1:2], 0.0))
            dve.wait_ge(sem("ctx_in"), 32)
            chained(ts(mfull, maski, 0.0, None, ALU.is_equal))
            ts(negrow, mfull[0:1], NEG, None, ALU.mult).then_inc(sem("ctx_ready"), 1)
            dve.wait_ge(sem("ctx_ready"), 1)
            chained(ts(mfull, mfull, -1.0, 1.0, ALU.mult, ALU.add))
            for k in range(KD):
                tt(ctxTm[:, :, k, :], ctxTm[:, :, k, :], mfull, ALU.mult).then_inc(sem("ctx_ready"), 1)

            def ln_stats(g, which, src):
                for j in range(GT):
                    dve.bn_stats(st[which][:, j, :], src[:, j, :]).then_inc(sem(f"bn{which}"), 1)
                for j in range(GT):
                    dve.wait_ge(sem(f"bn{which}"), GT * g + j + 1).then_inc(sem("passed"), 1)
                    ins = dve.bn_aggr(mv[which][:, j, :], st[which][:, j, :])
                ins.then_inc(sem(f"stats{which}"), 1)

            def ln_apply(g, which, dst, src, rstd_sem, done):
                dve.wait_ge(sem(rstd_sem), g + 1)
                for j in range(GT):
                    ts(dst[:, j, :], src[:, j, :], mv[which][:, j, 0:1], rstd[which][:, j:j + 1],
                       ALU.subtract, ALU.mult).then_inc(sem(done), 1)

            def ln1_stats(g, p, turns):
                dve.wait_ge(sem(f"x_in{p}"), (turns + 1) * 16).then_inc(sem("passed"), 1)
                ln_stats(g, 0, xin[p])

            def ln1_apply(g, p):
                if above_zero(KD * g):
                    dve.wait_ge(sem("t1_done"), KD * g)
                ln_apply(g, 0, n1, xin[p], "rstd_a", "n1_done")

            def row_max(g):
                dve.wait_ge(sem("s_done"), g + 1)
                if above_zero(GT * g):
                    dve.wait_ge(sem("probs_done"), GT * g)
                s = bank[:, 6, :].rearrange("p (j n) -> p j n", j=GT)[:, :, 0:KV]
                dve.tensor_reduce(negmax, s, AX.X, ALU.max, negate=True).then_inc(sem("negmax_done"), 1)

            def prob_scale(g):
                dve.wait_ge(sem("probs_done"), GT * (g + 1))
                dve.reciprocal(pscale, psums).then_inc(sem("pscale_done"), 1)
                dve.wait_ge(sem("pscale_done"), 2 * g + 1)
                ts(pscale, pscale, gains[:, 0:1], None, ALU.mult).then_inc(sem("pscale_done"), 1)

            def residual1(g, p, turns):
                dve.wait_ge(sem("pscale_done"), 2 * g + 2)
                if above_zero(turns * 16):
                    dve.wait_ge(sem(f"mid_out{p}"), turns * 16)
                for j in range(GT):
                    dve.wait_ge(sem("pv_done"), GT * g + (j // 2 + 1) * 2)
                    stt(x1[p][:, j, :], bank[:, 4 + j // 2, (j % 2) * D:(j % 2 + 1) * D], pscale[:, j:j + 1], xin[p][:, j, :],
                        ALU.mult, ALU.add).then_inc(sem("x1_done"), 1)

            def ln2_stats(g, p):
                for j in range(GT):
                    dve.wait_ge(sem("x1_done"), GT * g + j + 1).then_inc(sem("passed"), 1)
                    dve.bn_stats(st[1][:, j, :], x1[p][:, j, :]).then_inc(sem("bn1"), 1)
                for j in range(GT):
                    dve.wait_ge(sem("bn1"), GT * g + j + 1).then_inc(sem("passed"), 1)
                    ins = dve.bn_aggr(mv[1][:, j, :], st[1][:, j, :])
                ins.then_inc(sem("stats1"), 1)

            def ln2_apply(g, p, turns):
                if above_zero(turns * (2 * GT * 16)):
                    dve.wait_ge(sem(f"scattered{p}"), turns * (2 * GT * 16))
                ln_apply(g, 1, n2[p], x1[p], "rstd_b", "n2_done")

            def t2_low(g):
                for k in range(KD):
                    dve.wait_ge(sem("n2Th_done"), KD * g + k + 1)
                    tt(n2Tl[:, k, :], bank[:, 4 + k, :], n2Th[:, k, :], ALU.subtract).then_inc(sem("n2Tl_done"), 1)

            def hidden(f, m):
                dve.wait_ge(sem("silu_done"), MS * f + m + 1)
                stt(sil[m % 2], bank[:, 2 * (m % 2) + 1, :], bs13[:, 1, m:m + 1], sil[m % 2], ALU.add, ALU.mult)\
                    .then_inc(sem("h_done"), 1)

            def shared_out(f, p):
                dve.wait_ge(sem("d_done"), f + 1)
                stt(x1[p], bank[:, 0:GT, 0:D], gains[:, 2:3], x1[p], ALU.mult, ALU.add).then_inc(sem("shared_done"), 1)

            def route_a(f):
                dve.wait_ge(sem("gate_done"), f + 1)
                tt(logit, bank[:, 7, 0:GT * NE].rearrange("p (j e) -> p j e", j=GT),
                   gbias.unsqueeze(1).broadcast_to([P, GT, NE]), ALU.add).then_inc(sem("logit_done"), 1)
                dve.wait_ge(sem("logit_done"), f + 1).then_inc(sem("passed"), 1)
                for j in range(GT):
                    dve.max(top8[:, j, :], logit[:, j, :]).then_inc(sem("top_done"), 1)
                for j in range(GT):
                    dve.wait_ge(sem("top_done"), GT * f + j + 1).then_inc(sem("passed"), 1)
                    dve.max_index(top8i[:, j, :], top8[:, j, :], logit[:, j, :]).then_inc(sem("topi_done"), 1)
                m0 = top8[:, :, 0:1]
                tt(dlog[:, :, 0:NE], logit, m0.broadcast_to([P, GT, NE]), ALU.subtract)
                tt(dlog[:, :, NE:NE + 1], top8[:, :, 1:2], m0, ALU.subtract).then_inc(sem("dlog_done"), 1)

            def route_b(f):
                dve.wait_ge(sem("topi_done"), GT * (f + 1))
                for k in range(2):
                    tt(onehot[:, k, :, :], expert_no.unsqueeze(1).broadcast_to([P, GT, NE]),
                       top8i[:, :, k:k + 1].broadcast_to([P, GT, NE]), ALU.is_equal).then_inc(sem("onehot_done"), 1)
                dve.wait_ge(sem("topi_done"), GT * (f + 1)).then_inc(sem("passed"), 1)
                cp(expert_all[:, bass.ds(f, 1), :, :].rearrange("p a k j -> p (a k) j"),
                   top8i[:, :, 0:2].rearrange("p j k -> p k j")).then_inc(sem("route_kept"), 1)
                dve.wait_ge(sem("onehot_done"), 2 * (f + 1))
                tt(routed, onehot[:, 0, :, :], onehot[:, 1, :, :], ALU.add).then_inc(sem("routed_done"), 1)

            def route_c(f):
                dve.wait_ge(sem("elog_done"), f + 1)
                dve.tensor_reduce(esum, elog[:, :, 0:NE], AX.X, ALU.add).then_inc(sem("weights_step"), 1)
                dve.wait_ge(sem("weights_step"), 4 * f + 1)
                dve.reciprocal(esum, esum).then_inc(sem("weights_step"), 1)
                dve.wait_ge(sem("weights_step"), 4 * f + 2)
                ts(gatew[:, 0, :], esum, gains[:, 2:3], None, ALU.mult).then_inc(sem("weights_step"), 1)
                dve.wait_ge(sem("weights_step"), 4 * f + 3)
                tt(gatew[:, 1, :], gatew[:, 0, :], elog[:, :, NE], ALU.mult).then_inc(sem("weights_step"), 1)
                dve.wait_ge(sem("weights_step"), 4 * f + 4).then_inc(sem("passed"), 1)
                cp(gate_all[:, bass.ds(f, 1), :, :].rearrange("p a k j -> p (a k j)"), gatew.rearrange("p k j -> p (k j)"))\
                    .then_inc(sem("route_kept"), 1)

            def route_d(f, p, turns):
                dve.wait_ge(sem("rank_done"), f + 1)
                tt(rrow, bank[:, 7, 0:GT * NE].rearrange("p (j e) -> p j e", j=GT),
                   expert_row.unsqueeze(1).broadcast_to([P, GT, NE]), ALU.add).then_inc(sem("rrow_done"), 1)
                dve.tensor_reduce(rsum, routed.rearrange("p j e -> p e j"), AX.X, ALU.add).then_inc(sem("rsum_done"), 1)
                dve.wait_ge(sem("rrow_done"), f + 1)
                for k in range(2):
                    tt(rsel[:, k, :, :], onehot[:, k, :, :], rrow, ALU.mult).then_inc(sem("rsel_done"), 1)
                dve.wait_ge(sem("rsum_done"), f + 1)
                tt(rank_base, rank_base, rsum, ALU.add).then_inc(sem("base_done"), 1)
                dve.wait_ge(sem("rsel_done"), 2 * (f + 1))
                if above_zero(turns * (2 * GT * 16)):
                    dve.wait_ge(sem(f"scattered{p}"), turns * (2 * GT * 16))
                with nc.allow_low_precision(reason="sums of whole numbers below 2^24, converted at the end"):
                    dve.tensor_reduce(pos[p], rsel, AX.X, ALU.add).then_inc(sem("pos_done"), 1)
                dve.wait_ge(sem("pos_done"), f + 1).then_inc(sem("passed"), 1)
                cp(pos_all[:, bass.ds(f, 1), :, :].rearrange("p a k j -> p (a k j)"), pos[p].rearrange("p k j -> p (k j)"))\
                    .then_inc(sem("route_kept"), 1)

            def step(turn, attn=True, ffn=True, nxt=True):
                g, f, p = turn(), turn(-1), turn.slot()
                row_max(g)
                if nxt:
                    ln1_stats(g + 1, 1 - p, turn.before(1))
                if ffn:
                    route_a(f)
                prob_scale(g)
                if ffn:
                    hidden(f, 0)
                    route_b(f)
                if nxt:
                    ln1_apply(g + 1, 1 - p)
                if ffn:
                    hidden(f, 1)
                residual1(g, p, turn.before())
                ln2_stats(g, p)
                if ffn:
                    hidden(f, 2)
                    route_c(f)
                    route_d(f, 1 - p, turn.before(-1))
                ln2_apply(g, p, turn.before())
                if ffn:
                    hidden(f, 3)
                t2_low(g)
                if ffn:
                    shared_out(f, 1 - p)

            ln1_stats(0, 0, 0)
            dve.wait_ge(sem("pool_const"), 18)
            ln1_apply(0, 0)
            dve.wait_ge(sem("small_in"), 16 * 10)
            chained(cp(gwh, gwf))
            tt(gwl, gwf, gwh, ALU.subtract).then_inc(sem("bias_ready"), 1)
            for done, dst, src, up_, n in ((2, b13, b13f, upper16, 2 * NE), (3, b2, b2f, upper16, 2 * NE), (4, bs2, bs2f, upper2, 2)):
                w = dst.shape[1]
                low = lowf[0:n, 0:w]
                chained(cp(dst, src))
                chained(tt(low, src, dst, ALU.subtract))
                chained(ts(low, low, up_[:, 1:2], None, ALU.mult))
                stt(dst, dst, up_[:, 0:1], low, ALU.mult, ALU.add).then_inc(sem("bias_ready"), 1)
                dve.wait_ge(sem("bias_ready"), done)
            dve.wait_ge(sem("gains_done"), 1)
            chained(ts(fgain, gains[:, 3:4], DEQ * DEQ, None, ALU.mult))
            dve.memset(rank_base, 0.0).then_inc(sem("base_done"), 1)

            step(Turn(0, 2, 0), ffn=False)
            step(Turn(0, 2, 1))
            step(Turn(0, 2, 2))
            with dve.Fori(0, 2) as it:
                step(Turn(it, 2, 3))
                step(Turn(it, 2, 4))
            step(Turn(0, 2, 7), nxt=False)
            f = NG - 1
            route_a(f)
            hidden(f, 0)
            route_b(f)
            hidden(f, 1)
            route_d(f, 1, NG // 2 - 1)
            dve.wait_ge(sem("base_done"), NG + 1)
            for h in range(2):
                cp(rank16[:, h * NE:(h + 1) * NE], rank_base).then_inc(sem("rank16_done"), 1)
            hidden(f, 2)
            route_c(f)
            dve.wait_ge(sem("count_mm"), 1)
            tt(padpos, bank[:, 7, 8:8 + NE], pad_row, ALU.add).then_inc(sem("padpos_done"), 1)
            chained(ts(cnt_i[:, 0:1], bank[0:2 * NE, 7, 0:1], float(P - 1), None, ALU.add))
            chained(ts(cnt_i[:, 1:2], cnt_i[:, 0:1], 7, None, ALU.arith_shift_right))
            cp(cnt_f[:, 0:1], cnt_i[:, 1:2]).then_inc(sem("tiles_done"), 1)
            dve.wait_ge(sem("tiles_done"), 1)
            ts(shift8, cnt_f[0:NE, 0:1], -float(P), float(RC), ALU.mult, ALU.add).then_inc(sem("ge_done"), 1)
            hidden(f, 3)
            dve.wait_ge(sem("count_mm"), 2)
            chained(cp(cnt_f[:, 1:3], bank[0:2 * NE, 7, 0:2]))
            stt(row_shift, bank[:, 7, 16:16 + NE], float(P), expert_row, ALU.mult, ALU.subtract)\
                .then_inc(sem("row_shift_done"), 1)
            ts(ge_in, tile_no, cnt_f[:, 1:2], None, ALU.is_ge).then_inc(sem("ge_done"), 1)
            ts(ge_ex, tile_no, cnt_f[:, 2:3], None, ALU.is_ge).then_inc(sem("ge_done"), 1)
            dve.wait_ge(sem("ge_done"), 3)
            chained(tt(pick, ge_ex, ge_in, ALU.subtract))
            dve.wait_ge(sem("count_mm"), 3)
            ts(tile_expert, bank[0:1, 7, 0:NT], float(NE - 1), None, ALU.min).then_inc(sem("table_done"), 1)
            stt(tile_row, tile_no[0:1, :], float(P), bank[0:1, 7, 128:128 + NT], ALU.mult, ALU.add)\
                .then_inc(sem("table_done"), 1)
            shared_out(f, 1)

            def step2(t, x=True, h=True, th=True):
                p = t.slot() % 2
                if h:
                    dve.wait_ge(sem("silu2_done"), t(1))
                    tt(hid[p], hid[p], bank[:, p, F:2 * F], ALU.mult).then_inc(sem("hid_done"), 1)
                if x:
                    dve.wait_ge(sem("xTh_done"), t(3))
                    tt(xTl[p], bank[:, 4 + p, 0:KD * P], xTh[p], ALU.subtract).then_inc(sem("xTl_done"), 1)
                    if above_zero(t(-1)):
                        dve.wait_ge(sem("y_mm_done"), t(-1)).then_inc(sem("passed"), 1)
                    cp(sel[t.slot(2)], pick[:, bass.ds(t(2), 1)].broadcast_to([2 * NE, P])).then_inc(sem("sel_done"), 1)
                if th:
                    dve.wait_ge(sem("hTh_done"), t())
                    tt(hTl[1 - p], bank[:, 3 - p, 0:KD * P], hTh[1 - p], ALU.subtract).then_inc(sem("hTl_done"), 1)

            for s in range(2):
                dve.wait_ge(sem(f"mid_out{s}"), 16 * (NG // 2))
                dve.wait_ge(sem(f"scattered{s}"), NG // 2 * 2 * GT * 16)
            step2(Turn(0, 4, -2), h=False, th=False)
            step2(Turn(0, 4, -1), h=False, th=False)
            step2(Turn(0, 4, 0), th=False)
            for c in range(1, 6):
                step2(Turn(0, 4, c))
            with dve.Fori(0, (NT - 8) // 4) as it:
                for c in range(6, 10):
                    step2(Turn(it, 4, c))
            step2(Turn(0, 4, NT - 2), x=False)
            step2(Turn(0, 4, NT - 1), x=False)
            step2(Turn(0, 4, NT), x=False, h=False)

            def x2(b, c):
                if c == 0:
                    dve.wait_ge(sem("gathered"), 256 * (b + 1))
                    dve.wait_ge(sem("xa_in"), 16 * (b + 1))
                    dve.wait_ge(sem("gw3_done"), b + 1)
                for k in range(2):
                    for j in range(GT):
                        if k:
                            dve.wait_ge(sem("x2a_done"), (b * GB + c) * GT + j + 1)
                        stt(xa[:, c, j, :], yr[:, c, k, j, :], gw3[:, c, k, j:j + 1], xa[:, c, j, :], ALU.mult, ALU.add)\
                            .then_inc(sem("x2b_done" if k else "x2a_done"), 1)

            def ln3_stats(b):
                for n in range(GB * GT):
                    dve.wait_ge(sem("x2b_done"), GB * GT * b + n + 1).then_inc(sem("passed"), 1)
                    ins = dve.bn_stats(st3[0][:, n, :], xa[:, n // GT, n % GT, :])
                    ins.then_inc(sem("bn30"), 1)
                for n in range(GB * GT):
                    dve.wait_ge(sem("bn30"), GB * GT * b + n + 1).then_inc(sem("passed"), 1)
                    ins = dve.bn_aggr(mv3[0][:, n, :], st3[0][:, n, :])
                ins.then_inc(sem("stats30"), 1)

            def ln3_apply(b):
                dve.wait_ge(sem("rs30"), b + 1)
                if above_zero(GB * KD * b):
                    dve.wait_ge(sem("t3_done"), GB * KD * b)
                for n in range(GB * GT):
                    ts(n3[:, n // GT, n % GT, :], xa[:, n // GT, n % GT, :], mv3[0][:, n, 0:1], rs3[0][:, n:n + 1],
                       ALU.subtract, ALU.mult).then_inc(sem("n3_done"), 1)

            def gate_weights(b):
                cp(gw3, gate_all[:, bass.ds(b * GB, GB), :, :]).then_inc(sem("gw3_done"), 1)

            def kq_of(b):
                if above_zero(GB * b):
                    dve.wait_ge(sem("s3_done"), GB * b).then_inc(sem("passed"), 1)
                cp(kqb, kqT[:, :, bass.ds(b, 1), :].rearrange("p k a s -> p k (a s)")).then_inc(sem("kqb_done"), 1)

            def score_max(b):
                for c in range(GB):
                    dve.wait_ge(sem("s3_done"), GB * b + c + 1)
                    dve.tensor_reduce(smax2[:, c:c + 1], bank[0:KV, 4 + c, :], AX.X, ALU.max).then_inc(sem("smax_step"), 1)
                dve.wait_ge(sem("smax_step"), 6 * b + 2).then_inc(sem("passed"), 1)
                cp(sbias[:, 0:1], kbias[:, bass.ds(b, 1)]).then_inc(sem("smax_step"), 1)
                tt(smax, smax2[:, 0:1], smax2[:, 1:2], ALU.max).then_inc(sem("smax_step"), 1)
                dve.wait_ge(sem("smax_step"), 6 * b + 4)
                tt(smax, smax, sbias[:, 0:1], ALU.add).then_inc(sem("smax_step"), 1)
                dve.wait_ge(sem("smax_step"), 6 * b + 5)
                tt(sbias[:, 1:2], sbias[:, 0:1], smax, ALU.subtract).then_inc(sem("smax_step"), 1)
                dve.wait_ge(sem("smax_step"), 6 * b + 6)
                ts(sbias[:, 1:2], sbias[:, 1:2], 0.25, None, ALU.mult).then_inc(sem("sbias_done"), 1)

            def scaled_values(b):
                dve.wait_ge(sem("attn_done"), GB * (b + 1))
                tt(ssum, ssum2[:, 0:1], ssum2[:, 1:2], ALU.add).then_inc(sem("vscale_step"), 1)
                dve.wait_ge(sem("vscale_step"), 3 * b + 1)
                dve.reciprocal(ssum, ssum).then_inc(sem("vscale_step"), 1)
                dve.wait_ge(sem("vscale_step"), 3 * b + 2)
                ts(vscale[0:KV, :], ssum, gains[0:KV, 1:2], None, ALU.mult).then_inc(sem("vscale_step"), 1)
                dve.wait_ge(sem("vscale_step"), 3 * b + 3)
                if above_zero(GB * GT * b):
                    dve.wait_ge(sem("o_done"), GB * GT * b)
                ts(vob, vo[:, bass.ds(b, 1), :].rearrange("p a d -> p (a d)"), vscale, None, ALU.mult).then_inc(sem("vob_done"), 1)

            def residual3(b, c):
                base = 6 - 2 * c
                n = b * GB + c
                if above_zero(n - 1):
                    dve.wait_ge(sem("out_done"), n - 1)
                dve.wait_ge(sem("o_done"), GT * (n + 1))
                for h in range(2):
                    tt(xf[:, c, 2 * h:2 * h + 2, :].rearrange("p j d -> p (j d)"), bank[:, base + h, :],
                       xa[:, c, 2 * h:2 * h + 2, :].rearrange("p j d -> p (j d)"), ALU.add).then_inc(sem("x3_half"), 1)
                for j in range(GT):
                    dve.wait_ge(sem("x3_half"), 2 * n + j // 2 + 1).then_inc(sem("passed"), 1)
                    ins = dve.bn_stats(st3[1][:, c * GT + j, :], xf[:, c, j, :])
                    ins.then_inc(sem("bn31"), 1)
                for j in range(GT):
                    dve.wait_ge(sem("bn31"), GT * n + j + 1).then_inc(sem("passed"), 1)
                    ins = dve.bn_aggr(mv3[1][:, c * GT + j, :], st3[1][:, c * GT + j, :])
                    if j == 0:
                        ins.then_inc(sem("x3_done"), 1)
                ins.then_inc(sem("stats31"), 1)

            def ln4_apply(b, c):
                n = b * GB + c
                dve.wait_ge(sem("rs31"), n + 1)
                if above_zero(n):
                    dve.wait_ge(sem("t4_done"), n)
                for j in range(GT):
                    m = c * GT + j
                    ts(n4[:, j, :], xf[:, c, j, :], mv3[1][:, m, 0:1], rs3[1][:, m:m + 1], ALU.subtract, ALU.mult)\
                        .then_inc(sem("n4_done"), 1)

            def n4_low(b, c):
                base = 6 - 2 * c
                for k in range(KD):
                    dve.wait_ge(sem("n4Th_done"), KD * (b * GB + c) + k + 1)
                    tt(n4Tl[c][:, k, :], bank[:, base + k, :], n4Th[c][:, k, :], ALU.subtract).then_inc(sem("n4Tl_done"), 1)

            def hidden3(b, c, m):
                dve.wait_ge(sem("sl3_done"), (b * GB + c) * ML + m + 1)
                tt(sl3[m % 2], bank[:, 2 * (m % 2) + 1, :], sl3[m % 2], ALU.mult).then_inc(sem("g3_done"), 1)

            def final(b, c):
                dve.wait_ge(sem("d3_done"), b * GB + c + 1)
                if above_zero(16 * b):
                    dve.wait_ge(sem(f"out_out{c}"), 16 * b)
                stt(ost[c], bank[:, 0:GT, 0:D], fgain, xf[:, c, :, :], ALU.mult, ALU.add).then_inc(sem("out_done"), 1)

            def step3(b, nxt=True):
                residual3(b, 1)
                hidden3(b, 0, 0)
                hidden3(b, 0, 1)
                ln4_apply(b, 1)
                hidden3(b, 0, 2)
                n4_low(b, 1)
                if nxt:
                    gate_weights(b + 1)
                    x2(b + 1, 0)
                hidden3(b, 0, 3)
                hidden3(b, 0, 4)
                if nxt:
                    x2(b + 1, 1)
                hidden3(b, 0, 5)
                if nxt:
                    ln3_stats(b + 1)
                    kq_of(b + 1)
                    ln3_apply(b + 1)
                final(b, 0)
                hidden3(b, 1, 0)
                hidden3(b, 1, 1)
                if nxt:
                    score_max(b + 1)
                    scaled_values(b + 1)
                hidden3(b, 1, 2)
                hidden3(b, 1, 3)
                if nxt:
                    residual3(b + 1, 0)
                hidden3(b, 1, 4)
                hidden3(b, 1, 5)
                if nxt:
                    ln4_apply(b + 1, 0)
                    n4_low(b + 1, 0)
                final(b, 1)

            dve.wait_ge(sem("y_mm_done"), NT)
            dve.wait_ge(sem("kq_done"), 3)
            dve.wait_ge(sem("vo_done"), 2)
            chained(dve.memset(vscale, 0.0))
            chained(cp(vscale[96:97, :], gains[96:97, 1:2]))
            gate_weights(0)
            kq_of(0)
            x2(0, 0)
            x2(0, 1)
            ln3_stats(0)
            ln3_apply(0)
            score_max(0)
            scaled_values(0)
            residual3(0, 0)
            ln4_apply(0, 0)
            n4_low(0, 0)
            step3(0)
            with dve.Fori(1, B - 1) as b:
                step3(b)
            step3(B - 1, nxt=False)


def kernel(**inputs):
    import numpy as np
    import concourse.bacc as bacc
    from concourse.bass_utils import run_bass_kernel_spmd

    a = {k: np.asarray(v) for k, v in inputs.items()}

    def slices(w):
        k = w.shape[0] // P
        return w.reshape(k, P, w.shape[1]).transpose(1, 0, 2).reshape(P, -1)

    ctx = a["ctx_1024"]
    w1, w3, w2 = (a[f"L0_ffn_w{n}"] for n in (1, 3, 2))
    w13 = np.concatenate([w1.transpose(0, 2, 1), w3.transpose(0, 2, 1)], axis=2)
    wexp = np.stack([np.stack([w13[e, :P], w13[e, P:], slices(w2[e].T)]) for e in range(NE)])
    ws1, ws3, ws2 = (a[f"L0_ffn_ws{n}"].T for n in (1, 3, 2))
    wsh = np.stack([ws1[:P], ws1[P:], ws3[:P], ws3[P:], slices(ws2[:2 * P]), slices(ws2[2 * P:])])
    wint = np.concatenate([slices(a["L1_ffn_w_gate"].T), slices(a["L1_ffn_w_up"].T), slices(a["L1_ffn_w_down"].T)], axis=1)
    laid = {
        "x": a["x"].reshape(T, D),
        "ctx": ctx,
        "ctx_cols": ctx.reshape(B, KV, KD, P).transpose(3, 0, 2, 1).reshape(P, -1),
        "mask": a["mask_BxS2_ik1"],
        "g_xattn": a["g_xattn"],
        "g_ffn": a["g_ffn"],
        "wexp": wexp.reshape(-1, 512),
        "wsh": wsh.reshape(-1, 512),
        "b13": np.concatenate([a["L0_ffn_b1"], a["L0_ffn_b3"]], axis=1),
        "b2": a["L0_ffn_b2"],
        "bs13": np.stack([a["L0_ffn_bs1"].reshape(MS, P), a["L0_ffn_bs3"].reshape(MS, P)]).transpose(2, 0, 1).reshape(P, -1),
        "bs2": a["L0_ffn_bs2"],
        "gate_w": slices(a["L0_ffn_gate_w"].T),
        "gate_b": a["L0_ffn_gate_b"],
        "wk": slices(a["L1_xattn_Wk"]),
        "wv": slices(np.tile(a["L1_xattn_Wv"], (1, P // DH))),
        "wqT": a["L1_xattn_Wq"].T,
        "wo": slices(a["L1_xattn_Wo"]),
        "bqk": np.stack([a["L1_xattn_bq"], a["L1_xattn_bk"]], axis=1),
        "bv": np.tile(a["L1_xattn_bv"], P // DH).reshape(P, 1),
        "bo": a["L1_xattn_bo"].reshape(1, D),
        "wint": wint.reshape(P, 9, 512).transpose(1, 0, 2),
    }
    nc = bacc.Bacc("TRN2", target_bir_lowering=False, num_devices=1)
    arrays, given = {}, {}
    for name, v in laid.items():
        arrays[f"in_{name}"] = v = np.ascontiguousarray(v)
        given[name] = nc.dram_tensor(f"in_{name}", v.shape, mybir.dt.from_np(v.dtype), kind="ExternalInput").ap()
    out = nc.dram_tensor("out_0", (T, D), F32, kind="ExternalOutput").ap()
    flamingo_kernel(nc, given, out)
    r = run_bass_kernel_spmd(nc, [arrays], core_ids=[0])
    return r.results[0]["out_0"].reshape(B, S, D)
```

```python
from contextlib import ExitStack

import concourse.bass as bass
from concourse import mybir

B, S, D, KV = 4, 1024, 256, 77
NE, F = 8, 256
SF, LF = 512, 768
DH, NH = 16, 16
P = 128
KD = D // P
T = B * S
GT = 4
NG = T // (P * GT)
GB = NG // B
RC = T + P
NT = 2 * T // P + NE
SPARE = NE * RC
ROWS = SPARE + NE * P
MS, ML = SF // P, LF // P
EPS = 1e-5
NEG = -1e10
DEQ = 1.0 / 127.0

ALU = mybir.AluOpType
ACT = mybir.ActivationFunctionType
AX = mybir.AxisListType
F32 = mybir.dt.float32
F32R = mybir.dt.float32r
BF16 = mybir.dt.bfloat16
I32 = mybir.dt.int32
U32 = mybir.dt.uint32


def flamingo_kernel(nc, i, out):
    ctx = ExitStack()
    with ctx:
        sems = {}

        def sem(name):
            if name not in sems:
                sems[name] = ctx.enter_context(nc.semaphore(name))
            return sems[name]

        start = (nc.sbuf_base + 31) // 32 * 32

        class Area:
            def __init__(self, at, end):
                self.at, self.end = at, end

            def put(self, name, shape, dt):
                n = 1
                for s in shape[1:]:
                    n *= s
                size = (n * (2 if dt == BF16 else 4) + 31) // 32 * 32
                t = nc.alloc_sbuf_tensor_at(name, shape, dt, offset=self.at).ap()
                self.at += size
                assert self.at <= self.end, (name, self.at, self.end)
                return t

        top = nc.sbuf_usable_end // 32 * 32
        keep = Area(start, top)
        ident = keep.put("ident", [P, P], F32)
        tri = keep.put("tri", [P, P], BF16)
        onesb = keep.put("onesb", [P, P], BF16)
        onesf = keep.put("onesf", [1, P], F32)
        ones2 = keep.put("ones2", [2, P], F32R)
        ctxTm = keep.put("ctxTm", [P, B, KD, KV], F32)
        ctxr = keep.put("ctxr", [KV, B, D], F32)
        negrow = keep.put("negrow", [1, B, KV], F32)
        b13 = keep.put("b13", [2 * NE, 2 * F], F32R)
        b2 = keep.put("b2", [2 * NE, D], F32R)
        bs2 = keep.put("bs2", [2, D], F32R)
        bs13 = keep.put("bs13", [P, 2, MS], F32)
        gwh = keep.put("gwh", [P, KD, NE], F32R)
        gwl = keep.put("gwl", [P, KD, NE], F32R)
        gbias = keep.put("gbias", [P, NE], F32)
        gains = keep.put("gains", [P, 4], F32)
        fgain = keep.put("fgain", [P, 1], F32)
        halfpow = keep.put("halfpow", [P, 8], F32)
        upper16 = keep.put("upper16", [2 * NE, 2], F32)
        upper2 = keep.put("upper2", [2, 2], F32)
        expert_no = keep.put("expert_no", [P, NE], F32)
        expert_row = keep.put("expert_row", [P, NE], F32)
        tile_no = keep.put("tile_no", [2 * NE, NT], F32)
        incl = keep.put("incl", [NE, 2, NE], F32)
        excl = keep.put("excl", [NE, 2, NE], F32)
        rank_base = keep.put("rank_base", [P, NE], BF16)
        pos_all = keep.put("pos_all", [P, NG, 2, GT], F32)
        expert_all = keep.put("expert_all", [P, NG, 2, GT], F32)
        out_row = keep.put("out_row", [P, NG, 2, GT], U32)
        row_shift = keep.put("row_shift", [P, NE], F32)
        gate_all = keep.put("gate_all", [P, NG, 2, GT], F32)
        pick = keep.put("pick", [2 * NE, NT], F32)
        tile_expert = keep.put("tile_expert", [1, NT], I32)
        tile_row = keep.put("tile_row", [1, NT], I32)

        area_a = keep.at
        wa = Area(area_a, top)
        w13h = wa.put("w13h", [P, NE * KD, 2 * F], F32R)
        w13l = wa.put("w13l", [P, NE * KD, 2 * F], F32R)
        w2h = wa.put("w2h", [P, NE, KD * D], F32R)
        w2l = wa.put("w2l", [P, NE, KD * D], F32R)
        wsh = wa.put("wsh", [P, 6, 512], F32R)
        wsl = wa.put("wsl", [P, 6, 512], F32R)
        area_b = wa.at

        w1 = Area(area_b, top)
        xin = [w1.put(f"xin{p}", [P, GT, D], F32) for p in range(2)]
        n1 = w1.put("n1", [P, GT, D], F32)
        n1T = w1.put("n1T", [P, KD, GT * P], F32)
        probs = w1.put("probs", [P, GT, KV], F32)
        probsT = w1.put("probsT", [KV, GT * P], F32)
        stage = [w1.put(f"stage{c}", [P, 512], F32) for c in range(3)]
        area_b2 = w1.at
        x1 = [w1.put(f"x1{p}", [P, GT, D], F32) for p in range(2)]
        n2 = [w1.put(f"n2{p}", [P, GT, D], F32) for p in range(2)]
        n2Th = w1.put("n2Th", [P, KD, GT * P], F32R)
        n2Tl = w1.put("n2Tl", [P, KD, GT * P], F32R)
        sil = [w1.put(f"sil{p}", [P, 512], F32) for p in range(2)]
        hh = w1.put("hh", [P, MS, 512], F32R)
        hl = w1.put("hl", [P, MS, 512], F32R)
        negmax = w1.put("negmax", [P, GT], F32)
        psums = w1.put("psums", [P, GT], F32)
        pscale = w1.put("pscale", [P, GT], F32)
        st = [w1.put(f"st{p}", [P, GT, 6], F32) for p in range(2)]
        mv = [w1.put(f"mv{p}", [P, GT, 2], F32) for p in range(2)]
        ve = [w1.put(f"ve{p}", [P, GT], F32) for p in range(2)]
        rstd = [w1.put(f"rstd{p}", [P, GT], F32) for p in range(2)]
        logit = w1.put("logit", [P, GT, NE], F32)
        top8 = w1.put("top8", [P, GT, 8], F32)
        top8i = w1.put("top8i", [P, GT, 8], U32)
        dlog = w1.put("dlog", [P, GT, NE + 1], F32)
        elog = w1.put("elog", [P, GT, NE + 1], F32)
        esum = w1.put("esum", [P, GT], F32)
        onehot = w1.put("onehot", [P, 2, GT, NE], F32)
        routed = w1.put("routed", [P, GT, NE], BF16)
        rsum = w1.put("rsum", [P, NE], F32)
        rrow = w1.put("rrow", [P, GT, NE], F32)
        rsel = w1.put("rsel", [P, 2, GT, NE], F32)
        gatew = w1.put("gatew", [P, 2, GT], F32)
        pos = [w1.put(f"pos{p}", [P, 2, GT], U32) for p in range(2)]
        w0 = Area(area_b2, top)
        w0.put("raw_pad", [P, GT * D * 4], F32)
        b13f = w0.put("b13f", [2 * NE, 2 * F], F32)
        b2f = w0.put("b2f", [2 * NE, D], F32)
        bs2f = w0.put("bs2f", [2, D], F32)
        lowf = w0.put("lowf", [2 * NE, 2 * F], F32)
        gwf = w0.put("gwf", [P, KD, NE], F32)
        maski = w0.put("maski", [P, B, KV], I32)
        mfull = w0.put("mfull", [P, B, KV], F32)
        ints = w0.put("ints", [P, P], I32)
        gains_raw = w0.put("gains_raw", [P, 4], F32)
        assert w0.at <= w1.at

        c1 = Area(area_b, area_b2)
        ctxT = c1.put("ctxT", [P, B, KD, KV], F32)
        wk = c1.put("wk", [P, KD, DH], F32)
        wv = c1.put("wv", [P, KD, P], F32)
        wqT = c1.put("wqT", [DH, D], F32)
        wo = c1.put("wo", [P, KD, D], F32)
        bqk = c1.put("bqk", [DH, 2], F32)
        bvr = c1.put("bvr", [P, 1], F32)
        kT = c1.put("kT", [DH, B, KV], F32)
        vT = c1.put("vT", [P, B, KV], F32)
        kqT = c1.put("kqT", [P, KD, B, KV], F32)
        kbias = c1.put("kbias", [KV, B], F32)
        vo = c1.put("vo", [97, B, D], F32)
        zeros = c1.put("zeros", [P, D], F32)
        cnt_i = c1.put("cnt_i", [2 * NE, 2], I32)
        cnt_f = c1.put("cnt_f", [2 * NE, 4], F32)
        ge_in = c1.put("ge_in", [2 * NE, NT], F32)
        ge_ex = c1.put("ge_ex", [2 * NE, NT], F32)
        ones8 = c1.put("ones8", [NE, 1], F32)
        shift8 = c1.put("shift8", [NE, 1], F32)
        rank16 = c1.put("rank16", [P, 2 * NE], BF16)
        padpos = c1.put("padpos", [1, NE], I32)
        shifts = c1.put("shifts", [P, NE, NG * 2 * GT], F32)
        c2 = Area(area_b2, top)
        wint = c2.put("wint", [P, 9, 512], F32R)
        xg = [c2.put(f"xg{p}", [P, D], F32) for p in range(4)]
        yg = [c2.put(f"yg{p}", [P, D], F32) for p in range(4)]
        xTh = [c2.put(f"xTh{p}", [P, KD * P], F32R) for p in range(2)]
        xTl = [c2.put(f"xTl{p}", [P, KD * P], F32R) for p in range(2)]
        hid = [c2.put(f"hid{p}", [P, F], F32) for p in range(2)]
        hTh = [c2.put(f"hTh{p}", [P, KD * P], F32R) for p in range(2)]
        hTl = [c2.put(f"hTl{p}", [P, KD * P], F32R) for p in range(2)]
        sel = [c2.put(f"sel{p}", [2 * NE, P], F32R) for p in range(4)]
        wgv = wint[:, 0:3, :].rearrange("p a n -> p (a n)").rearrange("p (k n) -> p k n", k=KD)
        wuv = wint[:, 3:6, :].rearrange("p a n -> p (a n)").rearrange("p (k n) -> p k n", k=KD)
        wdv = wint[:, 6:9, :].rearrange("p a n -> p (a n)").rearrange("p (k n) -> p k n", k=ML)

        a3 = Area(area_a, area_b)
        xa = [a3.put(f"xa{p}", [P, GB, GT, D], F32) for p in range(3)]
        ost = [a3.put(f"ost{c}", [P, GT, D], F32) for c in range(GB)]
        yr = a3.put("yr", [P, GB, 2, GT, D], F32)
        n3 = a3.put("n3", [P, GB, GT, D], F32)
        n3T = a3.put("n3T", [P, KD, GB, GT * P], F32)
        attnT = a3.put("attnT", [97, GB, GT * P], F32)
        n4 = a3.put("n4", [P, GT, D], F32)
        n4Th = [a3.put(f"n4Th{c}", [P, KD, GT * P], F32R) for c in range(GB)]
        n4Tl = [a3.put(f"n4Tl{c}", [P, KD, GT * P], F32R) for c in range(GB)]
        sl3 = [a3.put(f"sl3{p}", [P, 512], F32) for p in range(2)]
        g3h = a3.put("g3h", [P, ML, 512], F32R)
        g3l = a3.put("g3l", [P, ML, 512], F32R)
        vob = a3.put("vob", [97, D], F32)
        vscale = a3.put("vscale", [97, 1], F32)
        smax2 = a3.put("smax2", [KV, GB], F32)
        smax = a3.put("smax", [KV, 1], F32)
        sbias = a3.put("sbias", [KV, 2], F32)
        ssum2 = a3.put("ssum2", [KV, GB], F32)
        ssum = a3.put("ssum", [KV, 1], F32)
        st3 = [a3.put(f"st3{c}", [P, GB * GT, 6], F32) for c in range(2)]
        mv3 = [a3.put(f"mv3{c}", [P, GB * GT, 2], F32) for c in range(2)]
        ve3 = [a3.put(f"ve3{c}", [P, GB * GT], F32) for c in range(2)]
        nb3 = [a3.put(f"nb3{c}", [P, GB * GT], F32) for c in range(2)]
        rs3 = [a3.put(f"rs3{c}", [P, GB * GT], F32) for c in range(2)]

        bank = ctx.enter_context(nc.psum_tensor("bank", [P, 8, 512], F32))

        xs = nc.dram_tensor("rows_by_expert", [ROWS, D], F32, kind="Internal").ap()
        ys = nc.dram_tensor("expert_out", [NT * P, D], F32, kind="Internal").ap()
        xmid = nc.dram_tensor("x_shared", [T, D], F32, kind="Internal").ap()

        def rows(t, g, n=GT):
            return t[bass.ds(g * (GT * P), n * P), :].rearrange("(j p) d -> p j d", p=P)

        def above_zero(n):
            return not isinstance(n, int) or n > 0


        class Turn:

            def __init__(self, loop, every, c, slots=None):
                self.loop, self.every, self.c, self.slots = loop, every, c, slots or every

            def __call__(self, k=0):
                return self.loop * self.every + (self.c + k)

            def before(self, k=0):
                return self.loop * (self.every // self.slots) + (self.c + k) // self.slots

            def slot(self, k=0):
                return (self.c + k) % self.slots

        POOL_LOWS = ML - 3 + ML

        def low_of(n):
            b, m = n // (GB * ML), n % (GB * ML)
            return ("low_vector", 3 * b + m + 1) if m < 3 else ("low_pool", POOL_LOWS * b + m - 2)

        block = ctx.enter_context(nc.Block())

        @block.sync
        def _(sp):
            def small(dst, src, name="small_in"):
                sp.dma_start(dst, src).then_inc(sem(name), 16)

            def load_x(g, p):
                if above_zero(GT * (g - 1)):
                    sp.wait_ge(sem("x1_done"), GT * (g - 1)).then_inc(sem("passed"), 1)
                sp.dma_start(xin[p], rows(i["x"], g)).then_inc(sem(f"x_in{p}"), 16)

            def load_expert(e):
                for c in range(3):
                    sp.wait_ge(sem(f"low_done{c}"), e + 2).then_inc(sem("passed"), 1)
                    src = i["wexp"][bass.ds(e * (3 * P) + c * P, P), :]
                    sp.dma_start(stage[c], src).then_inc(sem(f"stage_in{c}"), 16)

            def store_mid(f, p):
                sp.wait_ge(sem("shared_done"), 2 * f + 2).then_inc(sem("passed"), 1)
                sp.dma_start(rows(xmid, f), x1[p]).then_inc(sem(f"mid_out{p}"), 16)

            load_x(0, 0)
            small(ctxTm.rearrange("p b k s -> p (b k s)"), i["ctx_cols"], "ctx_in")
            small(maski, i["mask"].partition_broadcast(P), "ctx_in")
            for c in range(3):
                sp.dma_start(stage[c], i["wsh"][c * P:(c + 1) * P, :]).then_inc(sem(f"stage_in{c}"), 16)
            small(ctxr, i["ctx"].rearrange("b s d -> s b d"), "ctxr_in")
            small(gains_raw[:, 0:2], i["g_xattn"].partition_broadcast(P))
            small(gains_raw[:, 2:4], i["g_ffn"].partition_broadcast(P))
            small(gbias, i["gate_b"].partition_broadcast(P))
            small(gwf.rearrange("p k e -> p (k e)"), i["gate_w"])
            small(bs13.rearrange("p a m -> p (a m)"), i["bs13"])
            small(bs2f, i["bs2"].partition_broadcast(2))
            for h in range(2):
                small(b13f[h * NE:(h + 1) * NE, :], i["b13"])
                small(b2f[h * NE:(h + 1) * NE, :], i["b2"])
            load_x(1, 1)
            for c in range(3):
                sp.wait_ge(sem(f"low_done{c}"), 1)
                sp.dma_start(stage[c], i["wsh"][(c + 3) * P:(c + 4) * P, :]).then_inc(sem(f"stage_in{c}"), 16)

            def step(g, p, load=True, store=True):
                load_expert(g)
                if load:
                    load_x(g + 2, p)
                if store:
                    store_mid(g - 1, 1 - p)

            step(0, 0, store=False)
            step(1, 1)
            with sp.Fori(0, 2) as it:
                step(it * 2 + 2, 0)
                step(it * 2 + 3, 1)
            step(6, 0, load=False)
            step(7, 1, load=False)
            sp.wait_ge(sem("t2_done"), NG)
            sp.wait_ge(sem("x1_done"), GT * NG)
            for c in range(3):
                sp.wait_ge(sem(f"low_done{c}"), NG + 2)
            for dst, src in ((ctxT.rearrange("p b k s -> p (b k s)"), "ctx_cols"), (wk.rearrange("p k j -> p (k j)"), "wk"),
                             (wv.rearrange("p k j -> p (k j)"), "wv"), (wqT, "wqT"), (wo.rearrange("p k j -> p (k j)"), "wo"),
                             (bqk, "bqk"), (bvr, "bv")):
                small(dst, i[src], "l1_in")
            for b in range(B):
                small(vo[96:97, b, :], i["bo"], "l1_in")
            sp.wait_ge(sem("filled"), 1)
            small(xs[SPARE:ROWS, :].rearrange("(a p) d -> p a d", p=P),
                  zeros.unsqueeze(1).broadcast_to([P, NE, D]), "spare_out")
            sp.wait_ge(sem("padpos_done"), 1)
            for e in range(NE):
                row = sp.value_load(padpos[0:1, e:e + 1], min_val=0, max_val=SPARE - P)
                sp.dma_start(xs[bass.ds(row, P), :], zeros).then_inc(sem("pad_out"), 16)

            def load_tile(t, s):
                row = sp.value_load(tile_row[0:1, bass.ds(t, 1)], min_val=0, max_val=ROWS - P)
                if above_zero(t - 3):
                    sp.wait_ge(sem("tx_done"), t - 3).then_inc(sem("passed"), 1)
                sp.dma_start(xg[s], xs[bass.ds(row, P), :]).then_inc(sem(f"tile_in{s}"), 16)

            def store_tile(t, s):
                sp.wait_ge(sem("y_done"), t + 1).then_inc(sem("passed"), 1)
                sp.dma_start(ys[bass.ds(t * P, P), :], yg[s]).then_inc(sem(f"tile_out{s}"), 16)

            sp.wait_ge(sem("table_done"), 2)
            sp.wait_ge(sem("spare_out"), 16)
            for p in range(2):
                sp.wait_ge(sem(f"scattered{p}"), NG // 2 * 2 * GT * 16)
            sp.wait_ge(sem("pad_out"), 16 * NE)
            sp.wait_ge(sem("u_done"), MS * NG)
            sp.wait_ge(sem("gate_done"), NG)
            for t in range(4):
                load_tile(t, t)
            store_mid(7, 1)
            for t in range(4):
                load_tile(t + 4, t)
            with sp.Fori(0, NT // 4 - 2) as it:
                for r in range(4):
                    load_tile(it * 4 + 8 + r, r)
                    store_tile(it * 4 + r, r)
            for t in range(NT - 8, NT):
                store_tile(t, t % 4)

            def load_a(b):
                if b >= 3:
                    sp.wait_ge(sem("out_done"), 4 * (b - 2))
                sp.dma_start(xa[b % 3].rearrange("p c j d -> p (c j) d"), rows(xmid, b * GB, GB * GT))\
                    .then_inc(sem(f"xa_in{b % 2}"), 16)

            def store_out(u):
                sp.wait_ge(sem("out_done"), 2 * (u + 1))
                sp.dma_start(rows(out, u), ost[u % GB]).then_inc(sem(f"out_out{u % GB}"), 16)

            sp.wait_ge(sem("y_mm_done"), NT)
            load_a(0)
            load_a(1)
            for b in range(B):
                if b + 2 < B:
                    if b == 0:
                        sp.wait_ge(sem("xa_in0"), 16)
                    load_a(b + 2)
                store_out(b * GB)
                store_out(b * GB + 1)
            for c in range(GB):
                sp.wait_ge(sem(f"out_out{c}"), 16 * B)

        @block.gpsimd
        def _(pool):
            def chained(ins):
                pool_count[0] += 1
                ins.then_inc(sem("pool_const"), 1)
                pool.wait_ge(sem("pool_const"), pool_count[0])

            pool_count = [0]
            chained(pool.memset(ident, 0.0))
            chained(pool.affine_select(out=ident, in_=ident, compare_op=ALU.not_equal, fill=1.0, base=0,
                                       pattern=[[-1, P]], channel_multiplier=1))
            chained(pool.memset(halfpow, -0.5))
            chained(pool.memset(onesb, 1.0))
            chained(pool.memset(tri, 1.0))
            chained(pool.affine_select(out=tri, in_=tri, compare_op=ALU.is_gt, fill=0.0, base=0,
                                       pattern=[[1, P]], channel_multiplier=-1))
            for m, op in ((incl, ALU.is_ge), (excl, ALU.is_gt)):
                chained(pool.memset(m, 1.0))
                chained(pool.affine_select(out=m, in_=m, compare_op=op, fill=0.0, base=0,
                                           pattern=[[0, 2], [1, NE]], channel_multiplier=-1))
            for dst, pattern, mult, parts in ((expert_no, [[1, NE]], 0, P), (expert_row, [[RC, NE]], 0, P),
                                              (tile_no, [[1, NT]], 0, 2 * NE)):
                n = pattern[0][1]
                chained(pool.iota(ints[0:parts, 0:n], pattern, base=0, channel_multiplier=mult))
                chained(pool.tensor_copy(dst, ints[0:parts, 0:n]))

            def rstd_of(which, g, done):
                pool.wait_ge(sem(f"stats{which}"), g + 1).then_inc(sem("passed"), 1)
                pool.tensor_scalar(ve[which], mv[which][:, :, 1], EPS, None, ALU.add).then_inc(sem(f"var{which}"), 1)
                pool.wait_ge(sem(f"var{which}"), g + 1).then_inc(sem("passed"), 1)
                pool.tensor_tensor(rstd[which], ve[which], halfpow[:, 0:GT], ALU.pow).then_inc(sem(done), 1)

            def low_part(c, high, low, n):
                pool.wait_ge(sem(f"high_done{c}"), n).then_inc(sem("passed"), 1)
                pool.tensor_tensor(low, stage[c], high, ALU.subtract).then_inc(sem(f"low_done{c}"), 1)

            def expert_low(g, c):
                if c < 2:
                    high, low = (w[:, bass.ds(g * KD + c, 1), :].rearrange("p a n -> p (a n)") for w in (w13h, w13l))
                else:
                    high, low = (w[:, bass.ds(g, 1), :].rearrange("p a n -> p (a n)") for w in (w2h, w2l))
                low_part(c, high, low, g + 3)

            def hidden_low(f, m):
                pool.wait_ge(sem("hh_done"), MS * f + m + 1).then_inc(sem("passed"), 1)
                pool.tensor_tensor(hl[:, m, :], sil[m % 2], hh[:, m, :], ALU.subtract).then_inc(sem("hl_done"), 1)

            def scatter(f, p):
                pool.wait_ge(sem("pos_done"), f + 1).then_inc(sem("passed"), 1)
                for k in range(2):
                    for j in range(GT):
                        pool.indirect_dma_start(
                            out=xs, out_offset=bass.IndirectOffsetOnAxis(ap=pos[p][:, k, j:j + 1], axis=0),
                            in_=n2[p][:, j, :], in_offset=None).then_inc(sem(f"scattered{p}"), 16)

            def step(g, p, attn=True, ffn=True, nxt=True):
                f = g - 1
                if nxt:
                    rstd_of(0, g + 1, "rstd_a")
                if attn:
                    expert_low(g, 0)
                if ffn:
                    hidden_low(f, 0)
                if attn:
                    expert_low(g, 1)
                if ffn:
                    hidden_low(f, 1)
                if attn:
                    rstd_of(1, g, "rstd_b")
                    expert_low(g, 2)
                if ffn:
                    hidden_low(f, 2)
                    hidden_low(f, 3)
                    scatter(f, 1 - p)

            rstd_of(0, 0, "rstd_a")
            for r in range(2):
                for c in range(3):
                    low_part(c, wsh[:, 3 * r + c, :], wsl[:, 3 * r + c, :], r + 1)
            step(0, 0, ffn=False)
            step(1, 1)
            step(2, 0)
            with pool.Fori(0, 2) as it:
                step(it * 2 + 3, 1)
                step(it * 2 + 4, 0)
            step(7, 1, nxt=False)
            pool.wait_ge(sem("t2_done"), NG)
            pool.wait_ge(sem("x1_done"), GT * NG)
            pool.memset(zeros, 0.0).then_inc(sem("filled"), 1)
            pool.memset(ones8, 1.0).then_inc(sem("filled"), 1)
            pool.wait_ge(sem("filled"), 2)
            pool.memset(vo[64:96, :, :], 0.0).then_inc(sem("filled"), 1)
            pool.wait_ge(sem("filled"), 3)
            scatter(NG - 1, 1)
            pool.wait_ge(sem("shared_done"), 2 * NG)
            pool.wait_ge(sem("d_done"), 2 * NG)
            for p in range(2):
                pool.wait_ge(sem(f"scattered{p}"), NG // 2 * 2 * GT * 16)
                pool.wait_ge(sem(f"mid_out{p}"), 16 * (NG // 2))
            for c in range(3):
                pool.dma_start(wint[:, 3 * c:3 * c + 3, :], i["wint"][3 * c:3 * c + 3].rearrange("c p n -> p c n"))\
                    .then_inc(sem("wint_in"), 16)

            pool.wait_ge(sem("route_kept"), 3 * NG)
            pool.wait_ge(sem("row_shift_done"), 1)
            flat = [t.rearrange("p g k j -> p (g k j)") for t in (expert_all, pos_all, out_row)]
            for e in range(NE):
                pool.tensor_scalar(shifts[:, e, :], flat[0], float(e), row_shift[:, e:e + 1], ALU.is_equal, ALU.mult)\
                    .then_inc(sem("shifts_done"), 1)
            pool.wait_ge(sem("shifts_done"), NE)
            for n in (4, 2, 1):
                pool.tensor_tensor(shifts[:, 0:n, :], shifts[:, 0:n, :], shifts[:, n:2 * n, :], ALU.add)\
                    .then_inc(sem("shifts_done"), n)
                pool.wait_ge(sem("shifts_done"), NE + 8 - n)
            pool.tensor_tensor(shifts[:, 1, :], flat[1], shifts[:, 0, :], ALU.add).then_inc(sem("shifts_done"), 1)
            pool.wait_ge(sem("shifts_done"), 2 * NE)
            pool.tensor_copy(flat[2], shifts[:, 1, :]).then_inc(sem("shifts_done"), 1)
            pool.wait_ge(sem("shifts_done"), 2 * NE + 1)

            def gather(b, c, tiles):
                if b and tiles[0] == 0:
                    pool.wait_ge(sem("x2b_done"), GT * (b * GB + c - 1))
                for j in tiles:
                    for k in range(2):
                        pool.indirect_dma_start(
                            out=yr[:, c, k, j, :], out_offset=None, in_=ys,
                            in_offset=bass.IndirectOffsetOnAxis(ap=out_row[:, b * GB + c, k, j:j + 1], axis=0))\
                            .then_inc(sem(f"gathered{c}"), 16)

            def rstd3(which, u, used):
                r_ = slice(u % GB * GT, u % GB * GT + GT)
                pool.wait_ge(sem(f"stats3{which}"), u + 1)
                pool.tensor_scalar(ve3[which][:, r_], mv3[which][:, r_, 1], EPS, None, ALU.add).then_inc(sem(f"var3{which}"), 1)
                pool.wait_ge(sem(f"var3{which}"), u + 1)
                if u >= GB:
                    pool.wait_ge(sem(used), GT * (u - 1))
                pool.tensor_tensor(rs3[which][:, r_], ve3[which][:, r_], halfpow[:, 0:GT], ALU.pow)\
                    .then_inc(sem(f"rs3{which}"), 1)

            def low3(b, c, m):
                pool.wait_ge(sem("g3h_done"), (b * GB + c) * ML + m + 1)
                pool.tensor_tensor(g3l[:, m, :], sl3[m % 2], g3h[:, m, :], ALU.subtract).then_inc(sem("low_pool"), 1)

            pool.wait_ge(sem("y_mm_done"), NT)
            pool.wait_ge(sem("y_done"), NT)
            for s in range(4):
                pool.wait_ge(sem(f"tile_out{s}"), 16 * (NT // 4))
            gather(0, 0, range(GT))
            gather(0, 1, range(GT))
            rstd3(0, 0, "n3_done")
            rstd3(0, 1, "n3_done")
            pool.wait_ge(sem("rs30"), 2)
            pool.memset(attnT[64:96, :, :], 0.0).then_inc(sem("attn_pad"), 1)
            pool.wait_ge(sem("attn_pad"), 1)
            pool.memset(attnT[96:97, :, :], 1.0).then_inc(sem("attn_pad"), 1)
            pool.wait_ge(sem("attn_pad"), 2)
            gather(1, 0, range(GT))
            gather(1, 1, range(GT))
            rstd3(1, 0, "n4_done")
            rstd3(1, 1, "n4_done")
            rstd3(0, 2, "n3_done")
            for b in range(B):
                nxt, more = b + 1 < B, b + 2 < B
                u = (b + 1) * GB
                if more:
                    gather(b + 2, 0, range(2))
                if nxt:
                    rstd3(0, u + 1, "n3_done")
                if more:
                    gather(b + 2, 0, range(2, GT))
                for m in range(3, ML):
                    low3(b, 0, m)
                if more:
                    gather(b + 2, 1, range(GT))
                low3(b, 1, 0)
                low3(b, 1, 1)
                if nxt:
                    rstd3(1, u, "n4_done")
                low3(b, 1, 2)
                low3(b, 1, 3)
                if nxt:
                    rstd3(1, u + 1, "n4_done")
                low3(b, 1, 4)
                low3(b, 1, 5)
                if more:
                    rstd3(0, u + GB, "n3_done")

        @block.scalar
        def _(act):
            def copy(dst, src):
                return act.activation(dst, src, ACT.Copy)

            def stage_high(c, dst, n):
                act.wait_ge(sem(f"stage_in{c}"), 16 * n).then_inc(sem("passed"), 1)
                copy(dst, stage[c]).then_inc(sem(f"high_done{c}"), 1)

            def expert_high(g, c):
                if c < 2:
                    high = w13h[:, bass.ds(g * KD + c, 1), :].rearrange("p a n -> p (a n)")
                else:
                    high = w2h[:, bass.ds(g, 1), :].rearrange("p a n -> p (a n)")
                stage_high(c, high, g + 3)

            def t1_copy(g):
                if above_zero(g):
                    act.wait_ge(sem("s_done"), g)
                for k in range(KD):
                    act.wait_ge(sem("t1_done"), KD * g + k + 1)
                    copy(n1T[:, k, :], bank[:, 4 + k, :]).then_inc(sem("n1T_done"), 1)

            def softmax(g):
                act.wait_ge(sem("negmax_done"), g + 1)
                if above_zero(g):
                    act.wait_ge(sem("pt_done"), g)
                if above_zero(2 * g):
                    act.wait_ge(sem("pscale_done"), 2 * g)
                for j in range(GT):
                    act.activation(probs[:, j, :], bank[:, 6, j * P:j * P + KV], ACT.Exp, bias=negmax[:, j:j + 1],
                                   accum_out=psums[:, j:j + 1]).then_inc(sem("probs_done"), 1)

            def pt_copy(g):
                if above_zero(GT * g):
                    act.wait_ge(sem("pv_done"), GT * g)
                act.wait_ge(sem("pt_done"), g + 1)
                copy(probsT, bank[0:KV, 7, :]).then_inc(sem("probsT_done"), 1)

            def silu(f, m):
                act.wait_ge(sem("u_done"), MS * f + m + 1)
                if above_zero(MS * f + m - 1):
                    act.wait_ge(sem("hl_done"), MS * f + m - 1)
                act.activation(sil[m % 2], bank[:, 2 * (m % 2), :], ACT.Silu, bias=bs13[:, 0, m:m + 1])\
                    .then_inc(sem("silu_done"), 1)

            def hidden_high(f, m):
                act.wait_ge(sem("h_done"), MS * f + m + 1)
                if above_zero(f):
                    act.wait_ge(sem("d_done"), 2 * f)
                copy(hh[:, m, :], sil[m % 2]).then_inc(sem("hh_done"), 1)

            def t2_copy(g):
                act.wait_ge(sem("t2_done"), g + 1)
                for k in range(KD):
                    copy(n2Th[:, k, :], bank[:, 4 + k, :]).then_inc(sem("n2Th_done"), 1)

            def step(g, p, attn=True, ffn=True, nxt=True):
                f = g - 1
                if attn:
                    softmax(g)
                if ffn:
                    act.wait_ge(sem("dlog_done"), f + 1)
                    act.activation(elog, dlog, ACT.Exp).then_inc(sem("elog_done"), 1)
                if attn:
                    expert_high(g, 0)
                if ffn:
                    silu(f, 0)
                if attn:
                    pt_copy(g)
                if ffn:
                    hidden_high(f, 0)
                if attn:
                    expert_high(g, 1)
                if ffn:
                    for m in range(1, MS):
                        if nxt and m == MS - 1:
                            t1_copy(g + 1)
                        silu(f, m)
                        hidden_high(f, m)
                elif nxt:
                    t1_copy(g + 1)
                if attn:
                    expert_high(g, 2)
                    t2_copy(g)

            act.wait_ge(sem("small_in"), 16 * 10)
            act.activation(gains, gains_raw, ACT.Tanh).then_inc(sem("gains_done"), 1)
            for c in range(3):
                stage_high(c, wsh[:, c, :], 1)
            t1_copy(0)
            for c in range(3):
                stage_high(c, wsh[:, 3 + c, :], 2)
            step(0, 0, ffn=False)
            step(1, 1)
            step(2, 0)
            with act.Fori(0, 2) as it:
                step(it * 2 + 3, 1)
                step(it * 2 + 4, 0)
            step(7, 1, nxt=False)
            step(8, 0, attn=False, nxt=False)

            def step2(t, x=True, h=True, th=True, y=True):
                p = t.slot() % 2
                if h:
                    act.wait_ge(sem("hm_done"), t(1))
                    if above_zero(t(-1)):
                        act.wait_ge(sem("th_done"), t(-1))
                    act.activation(hid[p], bank[:, p, 0:F], ACT.Silu).then_inc(sem("silu2_done"), 1)
                if th:
                    act.wait_ge(sem("th_done"), t())
                    copy(hTh[1 - p], bank[:, 3 - p, 0:KD * P]).then_inc(sem("hTh_done"), 1)
                if x:
                    act.wait_ge(sem("tx_done"), t(3))
                    copy(xTh[p], bank[:, 4 + p, 0:KD * P]).then_inc(sem("xTh_done"), 1)
                if y:
                    s = t.slot(-2)
                    if above_zero(t.before(-2) * 16):
                        act.wait_ge(sem(f"tile_out{s}"), t.before(-2) * 16)
                    act.wait_ge(sem("y_mm_done"), t(-1))
                    copy(yg[s], bank[:, 6 + p, 0:D]).then_inc(sem("y_done"), 1)

            step2(Turn(0, 4, -2), h=False, th=False, y=False)
            step2(Turn(0, 4, -1), h=False, th=False, y=False)
            step2(Turn(0, 4, 0), th=False, y=False)
            step2(Turn(0, 4, 1), y=False)
            for c in range(2, 6):
                step2(Turn(0, 4, c))
            with act.Fori(0, (NT - 8) // 4) as it:
                for c in range(6, 10):
                    step2(Turn(it, 4, c))
            step2(Turn(0, 4, NT - 2), x=False)
            step2(Turn(0, 4, NT - 1), x=False)
            step2(Turn(0, 4, NT), x=False, h=False)
            step2(Turn(0, 4, NT + 1), x=False, h=False, th=False)

            def norm(which, u, src, dst, done, tiles):
                act.wait_ge(sem(f"nb3{which}"), u + 1)
                for j in tiles:
                    m = u % GB * GT + j
                    act.activation(dst[:, j, :], src[:, j, :], ACT.Identity, bias=nb3[which][:, m:m + 1],
                                   scale=rs3[which][:, m:m + 1]).then_inc(sem(done), 1)

            def norm3(u, tiles=range(GT)):
                if u >= GB:
                    act.wait_ge(sem("t3_done"), KD * (u - 1))
                norm(0, u, xa[u // GB % 3][:, u % GB], n3[:, u % GB], "n3_done", tiles)

            def norm4(u, tiles=range(GT)):
                if u:
                    act.wait_ge(sem("t4_done"), u)
                norm(1, u, xa[u // GB % 3][:, u % GB], n4, "n4_done", tiles)

            def copy_n3(u):
                if u >= GB:
                    act.wait_ge(sem("s3_done"), u - 1)
                for k in range(KD):
                    act.wait_ge(sem("t3_done"), KD * u + k + 1)
                    copy(n3T[:, k, u % GB, :], bank[:, 4 + 2 * (u % GB) + k, :]).then_inc(sem("n3T_done"), 1)

            def softmax3(b):
                act.wait_ge(sem("sbias_done"), b + 1)
                if b:
                    act.wait_ge(sem("o_done"), b * GB * GT)
                for c in range(GB):
                    act.activation(attnT[0:KV, c, :], bank[0:KV, 4 + c, :], ACT.Exp, scale=0.25, bias=sbias[:, 1:2],
                                   accum_out=ssum2[:, c:c + 1]).then_inc(sem("attn_done"), 1)

            def copy_n4(u):
                act.wait_ge(sem("t4_done"), u + 1)
                if u >= GB:
                    act.wait_ge(sem("u3_done"), ML * (u - 1))
                for k in range(KD):
                    copy(n4Th[u % GB][:, k, :], bank[:, 6 - 2 * (u % GB) + k, :]).then_inc(sem("n4Th_done"), 1)

            def hidden3(b, c, m, between=None):
                n = (b * GB + c) * ML + m
                act.wait_ge(sem("u3_done"), n + 1)
                if n >= 2:
                    name, count = low_of(n - 2)
                    act.wait_ge(sem(name), count)
                act.activation(sl3[m % 2], bank[:, 2 * (m % 2), :], ACT.Silu, scale=DEQ).then_inc(sem("sl3_done"), 1)
                if between:
                    norm_part, u, tiles = between
                    norm_part(u, tiles)
                act.wait_ge(sem("g3_done"), n + 1)
                if n >= ML:
                    act.wait_ge(sem("d3_done"), 2 * (b * GB + c))
                copy(g3h[:, m, :], sl3[m % 2]).then_inc(sem("g3h_done"), 1)

            act.wait_ge(sem("kv_mm"), 1)
            act.activation(kT.rearrange("j b s -> j (b s)"), bank[0:DH, 4, 0:B * KV], ACT.Identity, bias=bqk[:, 1:2])\
                .then_inc(sem("kT_done"), 1)
            act.activation(vT.rearrange("j b s -> j (b s)"), bank[:, 5, 0:B * KV], ACT.Identity, bias=bvr)\
                .then_inc(sem("kT_done"), 1)
            act.wait_ge(sem("kq_mm"), 1)
            for m in range(KD):
                copy(kqT[:, m, :, :].rearrange("p b s -> p (b s)"), bank[:, 6 * m, 0:B * KV]).then_inc(sem("kq_done"), 1)
            copy(kbias, bank[0:KV, 4, 0:B]).then_inc(sem("kq_done"), 1)
            act.wait_ge(sem("vo_mm"), 1)
            act.wait_ge(sem("filled"), 3)
            for h in range(2):
                copy(vo[0:KV, 2 * h:2 * h + 2, :].rearrange("p b d -> p (b d)"), bank[0:KV, 2 + h, :])\
                    .then_inc(sem("vo_done"), 1)

            act.wait_ge(sem("y_mm_done"), NT)
            norm3(0)
            copy_n3(0)
            norm3(1)
            copy_n3(1)
            act.wait_ge(sem("attn_pad"), 2)
            softmax3(0)
            norm4(0)
            copy_n4(0)
            for b in range(B):
                nxt = b + 1 < B
                u = (b + 1) * GB
                if b == 0:
                    norm4(1)
                first, second = range(2), range(2, GT)
                hidden3(b, 0, 0, nxt and (norm3, u, first))
                hidden3(b, 0, 1, nxt and (norm3, u, second))
                hidden3(b, 0, 2)
                if b == 0:
                    copy_n4(1)
                elif nxt:
                    copy_n3(u)
                hidden3(b, 0, 3, nxt and (norm3, u + 1, first))
                if b == 0:
                    copy_n3(u)
                hidden3(b, 0, 4, nxt and (norm3, u + 1, second))
                hidden3(b, 0, 5)
                if nxt:
                    copy_n3(u + 1)
                    softmax3(b + 1)
                for m in range(3):
                    hidden3(b, 1, m)
                hidden3(b, 1, 3, nxt and (norm4, u, first))
                hidden3(b, 1, 4, nxt and (norm4, u, second))
                hidden3(b, 1, 5)
                if nxt:
                    copy_n4(u)
                    norm4(u + 1)
                    copy_n4(u + 1)

        @block.tensor
        def _(pe):
            mm = pe.matmul

            def t1(g, rows_in):
                pe.wait_ge(sem("n1_done"), GT * (g + 1))
                if above_zero(GT * g):
                    pe.wait_ge(sem("x1_done"), GT * g)
                if above_zero(KD * (g - 1)):
                    pe.wait_ge(sem("n2Tl_done"), KD * (g - 1))
                for k in range(KD):
                    for j in range(GT):
                        last = pe.transpose(bank[:, 4 + k, j * P:(j + 1) * P], rows_in[:, j, k * P:(k + 1) * P], ident)
                    last.then_inc(sem("t1_done"), 1)

            def scores(g, b):
                pe.wait_ge(sem("n1T_done"), KD * (g + 1))
                if above_zero(GT * g):
                    pe.wait_ge(sem("probs_done"), GT * g)
                for j in range(GT):
                    o = bank[:, 6, j * P:j * P + KV]
                    for k in range(KD):
                        mm(o, n1T[:, k, j * P:(j + 1) * P], at(ctxTm, b, k), start=(k == 0), stop=False)
                    last = mm(o, onesf, negrow[0:1, bass.ds(b, 1), :].rearrange("p a s -> p (a s)"), start=False, stop=True)
                last.then_inc(sem("s_done"), 1)

            def at(t, b, k):
                return t[:, bass.ds(b, 1), k, :].rearrange("p a s -> p (a s)")

            def probs_t(g):
                pe.wait_ge(sem("probs_done"), GT * (g + 1))
                if above_zero(g):
                    pe.wait_ge(sem("logit_done"), g)
                for j in range(GT):
                    last = pe.transpose(bank[0:KV, 7, j * P:(j + 1) * P], probs[:, j, :], ident)
                last.then_inc(sem("pt_done"), 1)

            def values(g, b):
                pe.wait_ge(sem("probsT_done"), g + 1)
                if above_zero(KD * g):
                    pe.wait_ge(sem("n2Tl_done"), KD * g)
                for j in range(GT):
                    mm(bank[:, 4 + j // 2, (j % 2) * D:(j % 2 + 1) * D], probsT[:, j * P:(j + 1) * P],
                       ctxr[:, bass.ds(b, 1), :].rearrange("s a d -> s (a d)"), start=True, stop=True).then_inc(sem("pv_done"), 1)

            def t2(g, p, nxt):
                pe.wait_ge(sem("n2_done"), GT * (g + 1))
                pe.wait_ge(sem("n1T_done"), KD * (g + 2 if nxt else g + 1))
                pe.wait_ge(sem("x1_done"), GT * (g + 1))
                for k in range(KD):
                    for j in range(GT):
                        last = pe.transpose(bank[:, 4 + k, j * P:(j + 1) * P], n2[p][:, j, k * P:(k + 1) * P], ident)
                last.then_inc(sem("t2_done"), 1)

            def three(o, ah, al, bh, bl, first, final):
                mm(o, ah, bh, start=first, stop=False)
                mm(o, ah, bl, start=False, stop=False)
                return mm(o, al, bh, start=False, stop=final)

            def up(f, m):
                if m < 2:
                    if above_zero(2 * f):
                        pe.wait_ge(sem("shared_done"), 2 * f - 1 + m)
                    if m == 0:
                        pe.wait_ge(sem("n2Tl_done"), KD * (f + 1))
                        pe.wait_ge(sem("n2Th_done"), KD * (f + 1))
                else:
                    pe.wait_ge(sem("h_done"), MS * f + m - 1)
                for w in range(2):
                    o = bank[:, 2 * (m % 2) + w, :]
                    for k in range(KD):
                        c = KD * w + k
                        s = slice(m * P, (m + 1) * P)
                        last = three(o, wsh[:, c, s], wsl[:, c, s], n2Th[:, k, :], n2Tl[:, k, :], k == 0, k == KD - 1)
                last.then_inc(sem("u_done"), 1)

            def down(f, lo, hi):
                order = [(j, k) for j in range(GT) for k in range(lo, hi)] if lo else \
                    [(j, k) for k in range(lo, hi) for j in range(GT)]
                if lo == 0:
                    pe.wait_ge(sem("h_done"), MS * f + MS)
                waited = lo
                for j, k in order:
                    if k >= waited:
                        pe.wait_ge(sem("hh_done"), MS * f + k + 1)
                        pe.wait_ge(sem("hl_done"), MS * f + k + 1)
                        waited = k + 1
                    c, s = 4 + k // 2, slice((k % 2) * D, (k % 2 + 1) * D)
                    t = slice(j * P, (j + 1) * P)
                    o = bank[:, j, 0:D]
                    if k == 0:
                        mm(o, ones2, bs2, start=True, stop=False)
                    last = three(o, hh[:, k, t], hl[:, k, t], wsh[:, c, s], wsl[:, c, s], False, k == MS - 1)
                    if k == MS - 1 and j % 2:
                        last.then_inc(sem("d_done"), 1)

            def gate(g):
                pe.wait_ge(sem("n2Tl_done"), KD * (g + 1))
                pe.wait_ge(sem("n2Th_done"), KD * (g + 1))
                pe.wait_ge(sem("probsT_done"), g + 1)
                if above_zero(g):
                    pe.wait_ge(sem("rrow_done"), g)
                for j in range(GT):
                    t = slice(j * P, (j + 1) * P)
                    for k in range(KD):
                        last = three(bank[:, 7, j * NE:(j + 1) * NE], n2Th[:, k, t], n2Tl[:, k, t], gwh[:, k, :], gwl[:, k, :],
                                     k == 0, k == KD - 1)
                last.then_inc(sem("gate_done"), 1)

            def rank(f):
                pe.wait_ge(sem("routed_done"), f + 1)
                pe.wait_ge(sem("base_done"), f + 1)
                o = bank[:, 7, 0:GT * NE].rearrange("p (j e) -> p j e", j=GT)
                mm(o, tri, routed, start=True, stop=False)
                for j in range(GT - 1):
                    mm(o[:, j + 1:GT, :], onesb, routed[:, j:j + 1, :].broadcast_to([P, GT - 1 - j, NE]),
                       start=False, stop=False, skip_group_check=True)
                mm(o, onesb, rank_base.unsqueeze(1).broadcast_to([P, GT, NE]), start=False, stop=True).then_inc(sem("rank_done"), 1)

            def step(g, b, bn, p, attn=True, ffn=True, nxt=True):
                f = g - 1
                if ffn:
                    up(f, 0)
                if attn:
                    probs_t(g)
                if ffn:
                    up(f, 1)
                if attn:
                    values(g, b)
                if ffn:
                    up(f, 2)
                    if attn:
                        pe.wait_ge(sem("probsT_done"), g + 1)
                    rank(f)
                if nxt:
                    t1(g + 1, n1)
                if ffn:
                    up(f, 3)
                if nxt:
                    scores(g + 1, bn)
                if ffn:
                    down(f, 0, 2)
                if attn:
                    t2(g, p, nxt)
                if ffn:
                    down(f, 2, MS)
                if attn:
                    gate(g)

            pe.wait_ge(sem("pool_const"), 16)
            t1(0, n1)
            pe.wait_ge(sem("ctx_ready"), 3)
            scores(0, 0)
            pe.wait_ge(sem("ctxr_in"), 16)
            step(0, 0, 0, 0, ffn=False)
            for c in range(3):
                pe.wait_ge(sem(f"low_done{c}"), 2)
            pe.wait_ge(sem("bias_ready"), 4)
            step(1, 0, 1, 1)
            step(2, 1, 1, 0)
            with pe.Fori(0, 2) as it:
                step(it * 2 + 3, it + 1, it + 2, 1)
                step(it * 2 + 4, it + 2, it + 2, 0)
            step(7, 3, 3, 1, nxt=False)
            f = NG - 1
            up(f, 0)
            up(f, 1)
            rank(f)
            up(f, 2)
            pe.wait_ge(sem("base_done"), NG + 1)
            pe.wait_ge(sem("rank16_done"), 2)
            mm(bank[0:2 * NE, 7, 0:1], rank16, onesb[:, 0:1], start=True, stop=True)
            mm(bank[:, 7, 8:8 + NE], onesb, rank_base, start=True, stop=True).then_inc(sem("count_mm"), 1)
            up(f, 3)
            pe.wait_ge(sem("tiles_done"), 1)
            pe.wait_ge(sem("padpos_done"), 1)
            mm(bank[0:2 * NE, 7, 0:1], incl.rearrange("p a e -> p (a e)"), cnt_f[0:NE, 0:1], start=True, stop=True)
            mm(bank[0:2 * NE, 7, 1:2], excl.rearrange("p a e -> p (a e)"), cnt_f[0:NE, 0:1], start=True, stop=True)
            mm(bank[:, 7, 16:16 + NE], cnt_f[0:NE, 0:1].broadcast_to([NE, P]), excl[:, 0, :], start=True, stop=True)\
                .then_inc(sem("count_mm"), 1)
            down(f, 0, 2)
            pe.wait_ge(sem("ge_done"), 3)
            pe.wait_ge(sem("filled"), 2)
            mm(bank[0:1, 7, 0:NT], ones8, ge_in[0:NE, :], start=True, stop=True)
            mm(bank[0:1, 7, 128:128 + NT], shift8, ge_in[0:NE, :], start=True, stop=True).then_inc(sem("count_mm"), 1)
            down(f, 2, MS)

            pe.wait_ge(sem("n2Tl_done"), KD * NG)
            pe.wait_ge(sem("shared_done"), 2 * NG)
            def tx(t, q, turns):
                pe.wait_ge(sem(f"tile_in{q}"), turns * 16)
                if above_zero(t - 1):
                    pe.wait_ge(sem("xTl_done"), t - 1)
                for k in range(KD):
                    last = pe.transpose(bank[:, 4 + q % 2, k * P:(k + 1) * P], xg[q][:, k * P:(k + 1) * P], ident)
                last.then_inc(sem("tx_done"), 1)

            def th(t, q):
                p = q % 2
                pe.wait_ge(sem("hid_done"), t + 1)
                if above_zero(t - 1):
                    pe.wait_ge(sem("hTl_done"), t - 1)
                for k in range(KD):
                    last = pe.transpose(bank[:, 2 + p, k * P:(k + 1) * P], hid[p][:, k * P:(k + 1) * P], ident)
                last.then_inc(sem("th_done"), 1)

            def hidden(t, q, e):
                p = q % 2
                pe.wait_ge(sem("xTl_done"), t + 1)
                if above_zero(t - 1):
                    pe.wait_ge(sem("hid_done"), t - 1)
                pe.wait_ge(sem("sel_done"), t + 1)
                mm(bank[:, p, :], sel[q], b13, start=True, stop=False)
                for k in range(KD):
                    wh, wl = (w[:, bass.ds(e * KD + k, 1), :].rearrange("p a n -> p (a n)") for w in (w13h, w13l))
                    s = slice(k * P, (k + 1) * P)
                    last = three(bank[:, p, :], xTh[p][:, s], xTl[p][:, s], wh, wl, False, k == KD - 1)
                last.then_inc(sem("hm_done"), 1)

            def outp(t, q, e):
                p = q % 2
                pe.wait_ge(sem("hTl_done"), t + 1)
                if above_zero(t - 1):
                    pe.wait_ge(sem("y_done"), t - 1)
                mm(bank[:, 6 + p, 0:D], sel[q], b2, start=True, stop=False)
                for k in range(KD):
                    wh, wl = (w[:, bass.ds(e, 1), k * D:(k + 1) * D].rearrange("p a n -> p (a n)") for w in (w2h, w2l))
                    s = slice(k * P, (k + 1) * P)
                    last = three(bank[:, 6 + p, 0:D], hTh[p][:, s], hTl[p][:, s], wh, wl, False, k == KD - 1)
                last.then_inc(sem("y_mm_done"), 1)

            def expert_of(t):
                return pe.value_load(tile_expert[0:1, bass.ds(t, 1)], min_val=0, max_val=NE - 1)

            def step2(t, experts, x=True, h=True, hd=True, y=True, ahead=True):
                if h:
                    if t.c not in experts:
                        experts[t.c] = expert_of(t())
                    hidden(t(), t.slot(), experts[t.c])
                if ahead:
                    experts[t.c + 1] = expert_of(t(1))
                if y and t.c - 2 not in experts:
                    experts[t.c - 2] = expert_of(t(-2))
                if hd:
                    th(t(-1), t.slot(-1))
                if x:
                    tx(t(2), t.slot(2), t.before(2) + 1)
                if y:
                    outp(t(-2), t.slot(-2), experts[t.c - 2])

            UNROLL = 8
            pe.wait_ge(sem("table_done"), 2)
            experts = {}
            step2(Turn(0, 4, -2), experts, h=False, hd=False, y=False, ahead=False)
            step2(Turn(0, 4, -1), experts, h=False, hd=False, y=False)
            step2(Turn(0, 4, 0), experts, hd=False, y=False)
            step2(Turn(0, 4, 1), experts, y=False)
            for c in range(2, 6):
                step2(Turn(0, 4, c), experts, ahead=(c < 5))
            with pe.Fori(0, (NT - 8) // UNROLL) as it:
                experts = {}
                for c in range(6, 6 + UNROLL):
                    step2(Turn(it, UNROLL, c, 4), experts, ahead=(c < 5 + UNROLL))
            experts = {}
            step2(Turn(0, 4, NT - 2), experts, x=False)
            step2(Turn(0, 4, NT - 1), experts, x=False, ahead=False)
            step2(Turn(0, 4, NT), experts, x=False, h=False, ahead=False)
            step2(Turn(0, 4, NT + 1), experts, x=False, h=False, hd=False, ahead=False)

            pe.wait_ge(sem("l1_in"), 16 * 11)
            pe.wait_ge(sem("xTl_done"), NT)
            pe.wait_ge(sem("hTl_done"), NT)
            pe.wait_ge(sem("y_done"), NT)
            for k in range(KD):
                mm(bank[0:DH, 4, 0:B * KV], wk[:, k, :], ctxT[:, :, k, :], start=(k == 0), stop=(k == KD - 1))
            for k in range(KD):
                last = mm(bank[:, 5, 0:B * KV], wv[:, k, :], ctxT[:, :, k, :], start=(k == 0), stop=(k == KD - 1))
            last.then_inc(sem("kv_mm"), 1)
            pe.wait_ge(sem("kT_done"), 2)
            for m in range(KD):
                mm(bank[:, 6 * m, 0:B * KV], wqT[:, m * P:(m + 1) * P], kT.rearrange("j b s -> j (b s)"), start=True, stop=True)
            for b in range(B):
                last = mm(bank[0:KV, 4, b:b + 1], kT[:, b, :], bqk[:, 0:1], start=True, stop=True)
            last.then_inc(sem("kq_mm"), 1)
            for b in range(B):
                o = bank[0:KV, 2 + b // 2, (b % 2) * D:(b % 2 + 1) * D]
                for k in range(KD):
                    last = mm(o, vT[:, b, :], wo[:, k, :], start=(k == 0), stop=(k == KD - 1))
            last.then_inc(sem("vo_mm"), 1)
            pe.wait_ge(sem("vo_done"), 2)
            pe.wait_ge(sem("kq_done"), 3)

            def t3(u):
                pe.wait_ge(sem("n3_done"), GT * (u + 1))
                if u >= GB:
                    pe.wait_ge(sem("n4Tl_done"), KD * GB * (u // GB))
                for k in range(KD):
                    for j in range(GT):
                        last = pe.transpose(bank[:, 4 + 2 * (u % GB) + k, j * P:(j + 1) * P], n3[:, u % GB, j, k * P:(k + 1) * P],
                                            ident)
                    last.then_inc(sem("t3_done"), 1)

            def scores3(b):
                for c in range(GB):
                    pe.wait_ge(sem("n3T_done"), KD * (b * GB + c + 1))
                    for k in range(KD):
                        last = mm(bank[0:KV, 4 + c, :], kqT[:, k, b, :], n3T[:, k, c, :], start=(k == 0), stop=(k == KD - 1))
                    last.then_inc(sem("s3_done"), 1)

            def out3(b):
                pe.wait_ge(sem("vob_done"), b + 1)
                pe.wait_ge(sem("attn_done"), GB * (b + 1))
                for c in range(GB):
                    base = 6 - 2 * c
                    for j in range(GT):
                        mm(bank[:, base + j // 2, (j % 2) * D:(j % 2 + 1) * D], attnT[:, c, j * P:(j + 1) * P], vob,
                           start=True, stop=True).then_inc(sem("o_done"), 1)

            def t4(u):
                pe.wait_ge(sem("n4_done"), GT * (u + 1))
                pe.wait_ge(sem("x3_done"), u + 1)
                base = 6 - 2 * (u % GB)
                for k in range(KD):
                    for j in range(GT):
                        last = pe.transpose(bank[:, base + k, j * P:(j + 1) * P], n4[:, j, k * P:(k + 1) * P], ident)
                last.then_inc(sem("t4_done"), 1)

            def up3(b, c, m):
                n = (b * GB + c) * ML + m
                if m < 2:
                    if b + c:
                        pe.wait_ge(sem("out_done"), 2 * (b * GB + c) - 1 + m)
                    if m == 0:
                        pe.wait_ge(sem("n4Tl_done"), KD * (b * GB + c + 1))
                        pe.wait_ge(sem("n4Th_done"), KD * (b * GB + c + 1))
                else:
                    pe.wait_ge(sem("g3_done"), n - 1)
                for w, wt in enumerate((wgv, wuv)):
                    o = bank[:, 2 * (m % 2) + w, :]
                    for k in range(KD):
                        s = wt[:, k, m * P:(m + 1) * P]
                        mm(o, s, n4Th[c][:, k, :], start=(k == 0), stop=False)
                        last = mm(o, s, n4Tl[c][:, k, :], start=False, stop=(k == KD - 1))
                last.then_inc(sem("u3_done"), 1)

            def down3(b, c, last_part):
                n = (b * GB + c) * ML
                if last_part:
                    order = [(k, j) for j in range(GT) for k in range(ML - 2, ML)]
                else:
                    pe.wait_ge(sem("g3_done"), n + ML)
                    order = [(k, j) for k in range(ML - 2) for j in range(GT)]
                waited = order[0][0]
                for k, j in order:
                    if k >= waited:
                        pe.wait_ge(sem("g3h_done"), n + k + 1)
                        name, count = low_of(n + k)
                        pe.wait_ge(sem(name), count)
                        waited = k + 1
                    t = slice(j * P, (j + 1) * P)
                    mm(bank[:, j, 0:D], g3h[:, k, t], wdv[:, k, :], start=(k == 0), stop=False)
                    last = mm(bank[:, j, 0:D], g3l[:, k, t], wdv[:, k, :], start=False, stop=(k == ML - 1))
                    if k == ML - 1 and j % 2:
                        last.then_inc(sem("d3_done"), 1)

            t3(0)
            t3(1)
            scores3(0)
            pe.wait_ge(sem("attn_pad"), 2)
            out3(0)
            t4(0)
            pe.wait_ge(sem("wint_in"), 48)
            for b in range(B):
                nxt = b + 1 < B
                u = (b + 1) * GB
                for m in range(3):
                    up3(b, 0, m)
                if b == 0:
                    t4(1)
                if nxt and b:
                    t3(u)
                up3(b, 0, 3)
                if nxt and b == 0:
                    t3(u)
                for m in range(4, ML):
                    up3(b, 0, m)
                if nxt:
                    t3(u + 1)
                down3(b, 0, False)
                if nxt:
                    scores3(b + 1)
                down3(b, 0, True)
                up3(b, 1, 0)
                up3(b, 1, 1)
                if nxt:
                    out3(b + 1)
                for m in range(2, ML):
                    up3(b, 1, m)
                if nxt:
                    t4(u)
                down3(b, 1, False)
                down3(b, 1, True)
                if nxt:
                    t4(u + 1)

        @block.vector
        def _(dve):
            tt, ts, stt, cp = dve.tensor_tensor, dve.tensor_scalar, dve.scalar_tensor_tensor, dve.tensor_copy
            count = [0]

            def chained(ins):
                count[0] += 1
                ins.then_inc(sem("dve_const"), 1)
                dve.wait_ge(sem("dve_const"), count[0])

            chained(dve.memset(onesf, 1.0))
            chained(dve.memset(ones2.bitcast(F32), 1.0))
            for m, h in ((upper16, NE), (upper2, 1)):
                chained(dve.memset(m[:, 0:1], 0.0))
                chained(dve.memset(m[:, 1:2], 1.0))
                chained(dve.memset(m[0:h, 0:1], 1.0))
                chained(dve.memset(m[0:h, 1:2], 0.0))
            dve.wait_ge(sem("ctx_in"), 32)
            chained(ts(mfull, maski, 0.0, None, ALU.is_equal))
            ts(negrow, mfull[0:1], NEG, None, ALU.mult).then_inc(sem("ctx_ready"), 1)
            dve.wait_ge(sem("ctx_ready"), 1)
            chained(ts(mfull, mfull, -1.0, 1.0, ALU.mult, ALU.add))
            for k in range(KD):
                tt(ctxTm[:, :, k, :], ctxTm[:, :, k, :], mfull, ALU.mult).then_inc(sem("ctx_ready"), 1)

            def ln_stats(g, which, src):
                for j in range(GT):
                    dve.bn_stats(st[which][:, j, :], src[:, j, :]).then_inc(sem(f"bn{which}"), 1)
                for j in range(GT):
                    dve.wait_ge(sem(f"bn{which}"), GT * g + j + 1).then_inc(sem("passed"), 1)
                    ins = dve.bn_aggr(mv[which][:, j, :], st[which][:, j, :])
                ins.then_inc(sem(f"stats{which}"), 1)

            def ln_apply(g, which, dst, src, rstd_sem, done):
                dve.wait_ge(sem(rstd_sem), g + 1)
                for j in range(GT):
                    ts(dst[:, j, :], src[:, j, :], mv[which][:, j, 0:1], rstd[which][:, j:j + 1],
                       ALU.subtract, ALU.mult).then_inc(sem(done), 1)

            def ln1_stats(g, p, turns):
                dve.wait_ge(sem(f"x_in{p}"), (turns + 1) * 16).then_inc(sem("passed"), 1)
                ln_stats(g, 0, xin[p])

            def ln1_apply(g, p):
                if above_zero(KD * g):
                    dve.wait_ge(sem("t1_done"), KD * g)
                ln_apply(g, 0, n1, xin[p], "rstd_a", "n1_done")

            def row_max(g):
                dve.wait_ge(sem("s_done"), g + 1)
                if above_zero(GT * g):
                    dve.wait_ge(sem("probs_done"), GT * g)
                s = bank[:, 6, :].rearrange("p (j n) -> p j n", j=GT)[:, :, 0:KV]
                dve.tensor_reduce(negmax, s, AX.X, ALU.max, negate=True).then_inc(sem("negmax_done"), 1)

            def prob_scale(g):
                dve.wait_ge(sem("probs_done"), GT * (g + 1))
                dve.reciprocal(pscale, psums).then_inc(sem("pscale_done"), 1)
                dve.wait_ge(sem("pscale_done"), 2 * g + 1)
                ts(pscale, pscale, gains[:, 0:1], None, ALU.mult).then_inc(sem("pscale_done"), 1)

            def residual1(g, p, turns):
                dve.wait_ge(sem("pscale_done"), 2 * g + 2)
                if above_zero(turns * 16):
                    dve.wait_ge(sem(f"mid_out{p}"), turns * 16)
                for j in range(GT):
                    dve.wait_ge(sem("pv_done"), GT * g + (j // 2 + 1) * 2)
                    stt(x1[p][:, j, :], bank[:, 4 + j // 2, (j % 2) * D:(j % 2 + 1) * D], pscale[:, j:j + 1], xin[p][:, j, :],
                        ALU.mult, ALU.add).then_inc(sem("x1_done"), 1)

            def ln2_stats(g, p):
                for j in range(GT):
                    dve.wait_ge(sem("x1_done"), GT * g + j + 1).then_inc(sem("passed"), 1)
                    dve.bn_stats(st[1][:, j, :], x1[p][:, j, :]).then_inc(sem("bn1"), 1)
                for j in range(GT):
                    dve.wait_ge(sem("bn1"), GT * g + j + 1).then_inc(sem("passed"), 1)
                    ins = dve.bn_aggr(mv[1][:, j, :], st[1][:, j, :])
                ins.then_inc(sem("stats1"), 1)

            def ln2_apply(g, p, turns):
                if above_zero(turns * (2 * GT * 16)):
                    dve.wait_ge(sem(f"scattered{p}"), turns * (2 * GT * 16))
                ln_apply(g, 1, n2[p], x1[p], "rstd_b", "n2_done")

            def t2_low(g):
                for k in range(KD):
                    dve.wait_ge(sem("n2Th_done"), KD * g + k + 1)
                    tt(n2Tl[:, k, :], bank[:, 4 + k, :], n2Th[:, k, :], ALU.subtract).then_inc(sem("n2Tl_done"), 1)

            def hidden(f, m):
                dve.wait_ge(sem("silu_done"), MS * f + m + 1)
                stt(sil[m % 2], bank[:, 2 * (m % 2) + 1, :], bs13[:, 1, m:m + 1], sil[m % 2], ALU.add, ALU.mult)\
                    .then_inc(sem("h_done"), 1)

            def shared_out(f, p):
                for h in range(2):
                    j = slice(2 * h, 2 * h + 2)
                    dve.wait_ge(sem("d_done"), 2 * f + h + 1)
                    stt(x1[p][:, j, :], bank[:, j, 0:D], gains[:, 2:3], x1[p][:, j, :], ALU.mult, ALU.add)\
                        .then_inc(sem("shared_done"), 1)

            def route_a(f):
                dve.wait_ge(sem("gate_done"), f + 1)
                tt(logit, bank[:, 7, 0:GT * NE].rearrange("p (j e) -> p j e", j=GT),
                   gbias.unsqueeze(1).broadcast_to([P, GT, NE]), ALU.add).then_inc(sem("logit_done"), 1)
                dve.wait_ge(sem("logit_done"), f + 1).then_inc(sem("passed"), 1)
                for j in range(GT):
                    dve.max(top8[:, j, :], logit[:, j, :]).then_inc(sem("top_done"), 1)
                for j in range(GT):
                    dve.wait_ge(sem("top_done"), GT * f + j + 1).then_inc(sem("passed"), 1)
                    dve.max_index(top8i[:, j, :], top8[:, j, :], logit[:, j, :]).then_inc(sem("topi_done"), 1)
                m0 = top8[:, :, 0:1]
                tt(dlog[:, :, 0:NE], logit, m0.broadcast_to([P, GT, NE]), ALU.subtract)
                tt(dlog[:, :, NE:NE + 1], top8[:, :, 1:2], m0, ALU.subtract).then_inc(sem("dlog_done"), 1)

            def route_b(f):
                dve.wait_ge(sem("topi_done"), GT * (f + 1))
                for k in range(2):
                    tt(onehot[:, k, :, :], expert_no.unsqueeze(1).broadcast_to([P, GT, NE]),
                       top8i[:, :, k:k + 1].broadcast_to([P, GT, NE]), ALU.is_equal).then_inc(sem("onehot_done"), 1)
                dve.wait_ge(sem("topi_done"), GT * (f + 1)).then_inc(sem("passed"), 1)
                cp(expert_all[:, bass.ds(f, 1), :, :].rearrange("p a k j -> p (a k) j"),
                   top8i[:, :, 0:2].rearrange("p j k -> p k j")).then_inc(sem("route_kept"), 1)
                dve.wait_ge(sem("onehot_done"), 2 * (f + 1))
                tt(routed, onehot[:, 0, :, :], onehot[:, 1, :, :], ALU.add).then_inc(sem("routed_done"), 1)

            def route_c(f):
                dve.wait_ge(sem("elog_done"), f + 1)
                dve.tensor_reduce(esum, elog[:, :, 0:NE], AX.X, ALU.add).then_inc(sem("weights_step"), 1)
                dve.wait_ge(sem("weights_step"), 4 * f + 1)
                dve.reciprocal(esum, esum).then_inc(sem("weights_step"), 1)
                dve.wait_ge(sem("weights_step"), 4 * f + 2)
                ts(gatew[:, 0, :], esum, gains[:, 2:3], None, ALU.mult).then_inc(sem("weights_step"), 1)
                dve.wait_ge(sem("weights_step"), 4 * f + 3)
                tt(gatew[:, 1, :], gatew[:, 0, :], elog[:, :, NE], ALU.mult).then_inc(sem("weights_step"), 1)
                dve.wait_ge(sem("weights_step"), 4 * f + 4).then_inc(sem("passed"), 1)
                cp(gate_all[:, bass.ds(f, 1), :, :].rearrange("p a k j -> p (a k j)"), gatew.rearrange("p k j -> p (k j)"))\
                    .then_inc(sem("route_kept"), 1)

            def route_d(f, p, turns):
                dve.wait_ge(sem("rank_done"), f + 1)
                tt(rrow, bank[:, 7, 0:GT * NE].rearrange("p (j e) -> p j e", j=GT),
                   expert_row.unsqueeze(1).broadcast_to([P, GT, NE]), ALU.add).then_inc(sem("rrow_done"), 1)
                dve.tensor_reduce(rsum, routed.rearrange("p j e -> p e j"), AX.X, ALU.add).then_inc(sem("rsum_done"), 1)
                dve.wait_ge(sem("rrow_done"), f + 1)
                for k in range(2):
                    tt(rsel[:, k, :, :], onehot[:, k, :, :], rrow, ALU.mult).then_inc(sem("rsel_done"), 1)
                dve.wait_ge(sem("rsum_done"), f + 1)
                tt(rank_base, rank_base, rsum, ALU.add).then_inc(sem("base_done"), 1)
                dve.wait_ge(sem("rsel_done"), 2 * (f + 1))
                if above_zero(turns * (2 * GT * 16)):
                    dve.wait_ge(sem(f"scattered{p}"), turns * (2 * GT * 16))
                with nc.allow_low_precision(reason="sums of whole numbers below 2^24, converted at the end"):
                    dve.tensor_reduce(pos[p], rsel, AX.X, ALU.add).then_inc(sem("pos_done"), 1)
                dve.wait_ge(sem("pos_done"), f + 1).then_inc(sem("passed"), 1)
                cp(pos_all[:, bass.ds(f, 1), :, :].rearrange("p a k j -> p (a k j)"), pos[p].rearrange("p k j -> p (k j)"))\
                    .then_inc(sem("route_kept"), 1)

            def step(turn, attn=True, ffn=True, nxt=True):
                g, f, p = turn(), turn(-1), turn.slot()
                if ffn:
                    route_a(f)
                if nxt:
                    ln1_stats(g + 1, 1 - p, turn.before(1))
                prob_scale(g)
                if ffn:
                    hidden(f, 0)
                    route_b(f)
                if nxt:
                    ln1_apply(g + 1, 1 - p)
                if ffn:
                    hidden(f, 1)
                residual1(g, p, turn.before())
                ln2_stats(g, p)
                if ffn:
                    hidden(f, 2)
                    route_c(f)
                    route_d(f, 1 - p, turn.before(-1))
                ln2_apply(g, p, turn.before())
                if ffn:
                    hidden(f, 3)
                if nxt:
                    row_max(g + 1)
                t2_low(g)
                if ffn:
                    shared_out(f, 1 - p)

            ln1_stats(0, 0, 0)
            dve.wait_ge(sem("pool_const"), 16)
            ln1_apply(0, 0)
            dve.wait_ge(sem("small_in"), 16 * 10)
            chained(cp(gwh, gwf))
            tt(gwl, gwf, gwh, ALU.subtract).then_inc(sem("bias_ready"), 1)
            for done, dst, src, up_, n in ((2, b13, b13f, upper16, 2 * NE), (3, b2, b2f, upper16, 2 * NE), (4, bs2, bs2f, upper2, 2)):
                w = dst.shape[1]
                low = lowf[0:n, 0:w]
                chained(cp(dst, src))
                chained(tt(low, src, dst, ALU.subtract))
                chained(ts(low, low, up_[:, 1:2], None, ALU.mult))
                stt(dst, dst, up_[:, 0:1], low, ALU.mult, ALU.add).then_inc(sem("bias_ready"), 1)
                dve.wait_ge(sem("bias_ready"), done)
            dve.wait_ge(sem("gains_done"), 1)
            chained(ts(fgain, gains[:, 3:4], DEQ * DEQ, None, ALU.mult))
            dve.memset(rank_base, 0.0).then_inc(sem("base_done"), 1)

            row_max(0)
            step(Turn(0, 2, 0), ffn=False)
            step(Turn(0, 2, 1))
            step(Turn(0, 2, 2))
            with dve.Fori(0, 2) as it:
                step(Turn(it, 2, 3))
                step(Turn(it, 2, 4))
            step(Turn(0, 2, 7), nxt=False)
            f = NG - 1
            def hidden_low(m):
                dve.wait_ge(sem("hh_done"), MS * f + m + 1)
                tt(hl[:, m, :], sil[m % 2], hh[:, m, :], ALU.subtract).then_inc(sem("hl_done"), 1)

            route_a(f)
            hidden(f, 0)
            route_b(f)
            hidden(f, 1)
            hidden_low(0)
            route_d(f, 1, NG // 2 - 1)
            dve.wait_ge(sem("base_done"), NG + 1)
            for h in range(2):
                cp(rank16[:, h * NE:(h + 1) * NE], rank_base).then_inc(sem("rank16_done"), 1)
            hidden_low(1)
            hidden(f, 2)
            route_c(f)
            dve.wait_ge(sem("count_mm"), 1)
            tt(padpos, bank[0:1, 7, 8:8 + NE], expert_row[0:1], ALU.add).then_inc(sem("padpos_done"), 1)
            chained(ts(cnt_i[:, 0:1], bank[0:2 * NE, 7, 0:1], float(P - 1), None, ALU.add))
            chained(ts(cnt_i[:, 1:2], cnt_i[:, 0:1], 7, None, ALU.arith_shift_right))
            cp(cnt_f[:, 0:1], cnt_i[:, 1:2]).then_inc(sem("tiles_done"), 1)
            dve.wait_ge(sem("tiles_done"), 1)
            ts(shift8, cnt_f[0:NE, 0:1], -float(P), float(RC), ALU.mult, ALU.add).then_inc(sem("ge_done"), 1)
            hidden_low(2)
            hidden(f, 3)
            dve.wait_ge(sem("count_mm"), 2)
            chained(cp(cnt_f[:, 1:3], bank[0:2 * NE, 7, 0:2]))
            stt(row_shift, bank[:, 7, 16:16 + NE], float(P), expert_row, ALU.mult, ALU.subtract)\
                .then_inc(sem("row_shift_done"), 1)
            ts(ge_in, tile_no, cnt_f[:, 1:2], None, ALU.is_ge).then_inc(sem("ge_done"), 1)
            ts(ge_ex, tile_no, cnt_f[:, 2:3], None, ALU.is_ge).then_inc(sem("ge_done"), 1)
            dve.wait_ge(sem("ge_done"), 3)
            chained(tt(pick, ge_ex, ge_in, ALU.subtract))
            hidden_low(3)
            dve.wait_ge(sem("count_mm"), 3)
            ts(tile_expert, bank[0:1, 7, 0:NT], float(NE - 1), None, ALU.min).then_inc(sem("table_done"), 1)
            stt(tile_row, tile_no[0:1, :], float(P), bank[0:1, 7, 128:128 + NT], ALU.mult, ALU.add)\
                .then_inc(sem("table_done"), 1)
            shared_out(f, 1)

            def step2(t, x=True, h=True, th=True, choose=True):
                p = t.slot() % 2
                if choose:
                    if above_zero(t(-2)):
                        dve.wait_ge(sem("y_mm_done"), t(-2)).then_inc(sem("passed"), 1)
                    cp(sel[t.slot(1)], pick[:, bass.ds(t(1), 1)].broadcast_to([2 * NE, P])).then_inc(sem("sel_done"), 1)
                if h:
                    dve.wait_ge(sem("silu2_done"), t(1))
                    tt(hid[p], hid[p], bank[:, p, F:2 * F], ALU.mult).then_inc(sem("hid_done"), 1)
                if th:
                    dve.wait_ge(sem("hTh_done"), t())
                    tt(hTl[1 - p], bank[:, 3 - p, 0:KD * P], hTh[1 - p], ALU.subtract).then_inc(sem("hTl_done"), 1)
                if x:
                    dve.wait_ge(sem("xTh_done"), t(3))
                    tt(xTl[p], bank[:, 4 + p, 0:KD * P], xTh[p], ALU.subtract).then_inc(sem("xTl_done"), 1)

            step2(Turn(0, 4, -2), h=False, th=False, choose=False)
            step2(Turn(0, 4, -1), h=False, th=False)
            step2(Turn(0, 4, 0), th=False)
            for c in range(1, 6):
                step2(Turn(0, 4, c))
            with dve.Fori(0, (NT - 8) // 4) as it:
                for c in range(6, 10):
                    step2(Turn(it, 4, c))
            step2(Turn(0, 4, NT - 2), x=False)
            step2(Turn(0, 4, NT - 1), x=False, choose=False)
            step2(Turn(0, 4, NT), x=False, h=False, choose=False)

            def rows_of(u):
                return xa[u // GB % 3][:, u % GB]

            def x2(u, ks=(0, 1)):
                b, c = u // GB, u % GB
                if ks[0] == 0:
                    dve.wait_ge(sem(f"gathered{c}"), 128 * (b + 1))
                    dve.wait_ge(sem(f"xa_in{b % 2}"), 16 * (b // 2 + 1))
                for k in ks:
                    for j in range(GT):
                        if k:
                            dve.wait_ge(sem("x2a_done"), u * GT + j + 1)
                        stt(rows_of(u)[:, j, :], yr[:, c, k, j, :], gate_all[:, u, k, j:j + 1], rows_of(u)[:, j, :],
                            ALU.mult, ALU.add).then_inc(sem("x2b_done" if k else "x2a_done"), 1)

            def stats(which, u, written, counts):
                for j in range(GT):
                    dve.wait_ge(sem(written), counts[j])
                    dve.bn_stats(st3[which][:, u % GB * GT + j, :], rows_of(u)[:, j, :]).then_inc(sem(f"bn3{which}"), 1)
                for j in range(GT):
                    dve.wait_ge(sem(f"bn3{which}"), GT * u + j + 1)
                    ins = dve.bn_aggr(mv3[which][:, u % GB * GT + j, :], st3[which][:, u % GB * GT + j, :])
                ins.then_inc(sem(f"stats3{which}"), 1)

            def stats3(u):
                stats(0, u, "x2b_done", [GT * u + j + 1 for j in range(GT)])

            def stats4(u):
                stats(1, u, "x3_half", [2 * u + j // 2 + 1 for j in range(GT)])

            def shift3(which, u):
                r_ = slice(u % GB * GT, u % GB * GT + GT)
                dve.wait_ge(sem(f"rs3{which}"), u + 1)
                stt(nb3[which][:, r_], mv3[which][:, r_, 0], -1.0, rs3[which][:, r_], ALU.mult, ALU.mult)\
                    .then_inc(sem(f"nb3{which}"), 1)

            def score_max(b):
                for c in range(GB):
                    dve.wait_ge(sem("s3_done"), GB * b + c + 1)
                    dve.tensor_reduce(smax2[:, c:c + 1], bank[0:KV, 4 + c, :], AX.X, ALU.max).then_inc(sem("smax_step"), 1)
                dve.wait_ge(sem("smax_step"), 4 * b + 2)
                tt(smax, smax2[:, 0:1], smax2[:, 1:2], ALU.max).then_inc(sem("smax_step"), 1)
                dve.wait_ge(sem("smax_step"), 4 * b + 3)
                tt(sbias[:, 0:1], smax, kbias[:, b:b + 1], ALU.add).then_inc(sem("smax_step"), 1)
                dve.wait_ge(sem("smax_step"), 4 * b + 4)
                stt(sbias[:, 1:2], kbias[:, b:b + 1], 1.0, sbias[:, 0:1], ALU.mult, ALU.subtract).then_inc(sem("sbias_a"), 1)
                dve.wait_ge(sem("sbias_a"), b + 1)
                ts(sbias[:, 1:2], sbias[:, 1:2], 0.25, None, ALU.mult).then_inc(sem("sbias_done"), 1)

            def scaled_values(b):
                dve.wait_ge(sem("attn_done"), GB * (b + 1))
                tt(ssum, ssum2[:, 0:1], ssum2[:, 1:2], ALU.add).then_inc(sem("vscale_step"), 1)
                dve.wait_ge(sem("vscale_step"), 3 * b + 1)
                dve.reciprocal(ssum, ssum).then_inc(sem("vscale_step"), 1)
                dve.wait_ge(sem("vscale_step"), 3 * b + 2)
                ts(vscale[0:KV, :], ssum, gains[0:KV, 1:2], None, ALU.mult).then_inc(sem("vscale_step"), 1)
                dve.wait_ge(sem("vscale_step"), 3 * b + 3)
                if b:
                    dve.wait_ge(sem("o_done"), GB * GT * b)
                ts(vob, vo[:, b, :], vscale, None, ALU.mult).then_inc(sem("vob_done"), 1)

            def residual3(u):
                base = 6 - 2 * (u % GB)
                dve.wait_ge(sem("o_done"), GT * (u + 1))
                dve.wait_ge(sem("n3_done"), GT * (u + 1))
                for h in range(2):
                    x = rows_of(u)[:, 2 * h:2 * h + 2, :].rearrange("p j d -> p (j d)")
                    ins = tt(x, bank[:, base + h, :], x, ALU.add)
                    ins.then_inc(sem("x3_half"), 1)

            def x3_read(u):
                dve.wait_ge(sem("x3_half"), 2 * u + 2).then_inc(sem("x3_done"), 1)

            def n4_low(u):
                base = 6 - 2 * (u % GB)
                for k in range(KD):
                    dve.wait_ge(sem("n4Th_done"), KD * u + k + 1)
                    tt(n4Tl[u % GB][:, k, :], bank[:, base + k, :], n4Th[u % GB][:, k, :], ALU.subtract)\
                        .then_inc(sem("n4Tl_done"), 1)

            def hidden3(b, c, m):
                dve.wait_ge(sem("sl3_done"), (b * GB + c) * ML + m + 1)
                tt(sl3[m % 2], bank[:, 2 * (m % 2) + 1, :], sl3[m % 2], ALU.mult).then_inc(sem("g3_done"), 1)

            def low3(b, m):
                dve.wait_ge(sem("g3h_done"), b * GB * ML + m + 1)
                tt(g3l[:, m, :], sl3[m % 2], g3h[:, m, :], ALU.subtract).then_inc(sem("low_vector"), 1)

            def final(u):
                c = u % GB
                if u >= GB:
                    dve.wait_ge(sem(f"out_out{c}"), 16 * (u // GB))
                for h in range(2):
                    j = slice(2 * h, 2 * h + 2)
                    dve.wait_ge(sem("d3_done"), 2 * u + h + 1)
                    stt(ost[c][:, j, :], bank[:, j, 0:D], fgain, rows_of(u)[:, j, :], ALU.mult, ALU.add)\
                        .then_inc(sem("out_done"), 1)

            dve.wait_ge(sem("y_mm_done"), NT)
            dve.wait_ge(sem("route_kept"), 3 * NG)
            chained(dve.memset(vscale, 0.0))
            chained(cp(vscale[96:97, :], gains[96:97, 1:2]))
            for u in range(GB):
                x2(u)
                stats3(u)
                shift3(0, u)
            dve.wait_ge(sem("kq_done"), 3)
            dve.wait_ge(sem("vo_done"), 2)
            score_max(0)
            x2(2, (0,))
            scaled_values(0)
            x2(2, (1,))
            for u in range(GB):
                residual3(u)
                stats4(u)
                x3_read(u)
            shift3(1, 0)
            stats3(2)
            shift3(1, 1)
            x2(3, (0,))
            n4_low(0)
            for b in range(B):
                nxt, more = b + 1 < B, b + 2 < B
                u = (b + 1) * GB
                if nxt:
                    shift3(0, u)
                hidden3(b, 0, 0)
                if nxt:
                    x2(u + 1, (1,))
                hidden3(b, 0, 1)
                low3(b, 0)
                if nxt:
                    stats3(u + 1)
                hidden3(b, 0, 2)
                low3(b, 1)
                if b == 0:
                    n4_low(1)
                if nxt:
                    shift3(0, u + 1)
                hidden3(b, 0, 3)
                low3(b, 2)
                hidden3(b, 0, 4)
                hidden3(b, 0, 5)
                if nxt:
                    score_max(b + 1)
                final(b * GB)
                if nxt:
                    scaled_values(b + 1)
                hidden3(b, 1, 0)
                hidden3(b, 1, 1)
                if more:
                    x2(u + GB, (0,))
                if nxt:
                    residual3(u)
                    stats4(u)
                    x3_read(u)
                hidden3(b, 1, 2)
                if nxt:
                    shift3(1, u)
                    residual3(u + 1)
                hidden3(b, 1, 3)
                if nxt:
                    stats4(u + 1)
                    x3_read(u + 1)
                hidden3(b, 1, 4)
                if more:
                    x2(u + GB, (1,))
                if nxt:
                    shift3(1, u + 1)
                hidden3(b, 1, 5)
                if nxt:
                    n4_low(u)
                if more:
                    stats3(u + GB)
                    x2(u + GB + 1, (0,))
                final(b * GB + 1)
                if nxt:
                    n4_low(u + 1)


def kernel(**inputs):
    import numpy as np
    import concourse.bacc as bacc
    from concourse.bass_utils import run_bass_kernel_spmd

    a = {k: np.asarray(v) for k, v in inputs.items()}

    def slices(w):
        k = w.shape[0] // P
        return w.reshape(k, P, w.shape[1]).transpose(1, 0, 2).reshape(P, -1)

    ctx = a["ctx_1024"]
    w1, w3, w2 = (a[f"L0_ffn_w{n}"] for n in (1, 3, 2))
    w13 = np.concatenate([w1.transpose(0, 2, 1), w3.transpose(0, 2, 1)], axis=2)
    wexp = np.stack([np.stack([w13[e, :P], w13[e, P:], slices(w2[e].T)]) for e in range(NE)])
    ws1, ws3, ws2 = (a[f"L0_ffn_ws{n}"].T for n in (1, 3, 2))
    wsh = np.stack([ws1[:P], ws1[P:], ws3[:P], ws3[P:], slices(ws2[:2 * P]), slices(ws2[2 * P:])])
    wint = np.concatenate([slices(a["L1_ffn_w_gate"].T), slices(a["L1_ffn_w_up"].T), slices(a["L1_ffn_w_down"].T)], axis=1)
    laid = {
        "x": a["x"].reshape(T, D),
        "ctx": ctx,
        "ctx_cols": ctx.reshape(B, KV, KD, P).transpose(3, 0, 2, 1).reshape(P, -1),
        "mask": a["mask_BxS2_ik1"],
        "g_xattn": a["g_xattn"],
        "g_ffn": a["g_ffn"],
        "wexp": wexp.reshape(-1, 512),
        "wsh": wsh.reshape(-1, 512),
        "b13": np.concatenate([a["L0_ffn_b1"], a["L0_ffn_b3"]], axis=1),
        "b2": a["L0_ffn_b2"],
        "bs13": np.stack([a["L0_ffn_bs1"].reshape(MS, P), a["L0_ffn_bs3"].reshape(MS, P)]).transpose(2, 0, 1).reshape(P, -1),
        "bs2": a["L0_ffn_bs2"],
        "gate_w": slices(a["L0_ffn_gate_w"].T),
        "gate_b": a["L0_ffn_gate_b"],
        "wk": slices(a["L1_xattn_Wk"]),
        "wv": slices(np.tile(a["L1_xattn_Wv"], (1, P // DH))),
        "wqT": a["L1_xattn_Wq"].T,
        "wo": slices(a["L1_xattn_Wo"]),
        "bqk": np.stack([a["L1_xattn_bq"], a["L1_xattn_bk"]], axis=1),
        "bv": np.tile(a["L1_xattn_bv"], P // DH).reshape(P, 1),
        "bo": a["L1_xattn_bo"].reshape(1, D),
        "wint": wint.reshape(P, 9, 512).transpose(1, 0, 2),
    }
    nc = bacc.Bacc("TRN2", target_bir_lowering=False, num_devices=1)
    arrays, given = {}, {}
    for name, v in laid.items():
        arrays[f"in_{name}"] = v = np.ascontiguousarray(v)
        given[name] = nc.dram_tensor(f"in_{name}", v.shape, mybir.dt.from_np(v.dtype), kind="ExternalInput").ap()
    out = nc.dram_tensor("out_0", (T, D), F32, kind="ExternalOutput").ap()
    flamingo_kernel(nc, given, out)
    r = run_bass_kernel_spmd(nc, [arrays], core_ids=[0])
    return r.results[0]["out_0"].reshape(B, S, D)
```
